# Optimizing a Trainium2 kernel written in Bass

```python
import numpy as np
import jax
import jax.numpy as jnp

def _softmax(x, axis=-1):
    return jax.nn.softmax(x, axis=axis)

def _gelu(x):
    return jax.nn.gelu(x, approximate=True)

def _silu(x):
    return jax.nn.silu(x)

def _sigmoid(x):
    return jax.nn.sigmoid(x)

def _layernorm(x, axis=-1, eps=1e-05):
    m = jnp.mean(x, axis=axis, keepdims=True)
    v = jnp.var(x, axis=axis, keepdims=True)
    return (x - m) / jnp.sqrt(v + eps)

def _scatter_add(tgt, idx, src, axis=0):
    return tgt.at[idx].add(src)

def _segment_sum(src, seg, n):
    return jax.ops.segment_sum(src, seg, n)
kernel_name = 'mk_xattn_ffn_d2_seqx_r8_af16db'

def setup_inputs(seed: int=0):
    np.random.seed(seed)
    _w = jnp.asarray

    def _rec_inputs():
        import jax
        import jax.numpy as jnp
        _rk = jax.random.key(seed)
        x = 7.22e-05 + 1 * jax.random.normal(jax.random.fold_in(_rk, 1), (32, 128, 128), jnp.float32)
        _lenS = 128 - jax.random.randint(jax.random.fold_in(_rk, 7), (32,), 0, max(1, 128 // 4) + 1, jnp.int32)
        _lenS2 = 128 - jax.random.randint(jax.random.fold_in(_rk, 8), (32,), 0, max(1, 128 // 4) + 1, jnp.int32)
        _ctx_1024P = jax.random.normal(jax.random.fold_in(_rk, 11), (32, 16, 128), jnp.float32)
        _ctx_1024c = jax.random.dirichlet(jax.random.fold_in(_rk, 511), 0.3 * jnp.ones((16,), jnp.float32), (32, 128))
        _ctx_1024t = jnp.einsum('bsk,bkd->bsd', _ctx_1024c, _ctx_1024P)
        _ctx_1024t = _ctx_1024t * jax.lax.rsqrt(jnp.mean(jnp.square(_ctx_1024t)) + 1e-12) * 0.953939
        ctx_1024 = 4.13588e-05 + 0.999923 * (_ctx_1024t + 0.3 * jax.random.normal(jax.random.fold_in(_rk, 611), (32, 128, 128), jnp.float32))
        _validS = jnp.arange(128)[None, :] < _lenS[:, None]
        _validS2 = jnp.arange(128)[None, :] < _lenS2[:, None]
        _causal = jnp.tril(jnp.ones((128, 128), dtype=bool))
        mask_BxS2_fk1 = jnp.where(jnp.broadcast_to(_validS2[:, :], (32, 128)), 1.0, 0.0).astype(jnp.float32)
        return (x, ctx_1024, mask_BxS2_fk1)
    x, ctx_1024, mask_BxS2_fk1 = _rec_inputs()

    def _L0_xattn_setup():
        import jax, jax.numpy as jnp
        import numpy as np
        D_MODEL = 128
        NHEAD = 16
        HEAD_DIM = D_MODEL // NHEAD
        key = jax.random.key(seed)
        ks = jax.random.split(key, 11)
        B, S, D = (4, 256, D_MODEL)
        scale = 1.0 / np.sqrt(D)
        inp = {'q': jax.random.normal(ks[0], (B, S, D), jnp.float32), 'k': jax.random.normal(ks[1], (B, S, D), jnp.float32), 'v': jax.random.normal(ks[2], (B, S, D), jnp.float32), 'Wq': jax.random.normal(ks[3], (D, D), jnp.float32) * scale, 'bq': jnp.zeros((D,), jnp.float32), 'Wk': jax.random.normal(ks[4], (D, D), jnp.float32) * scale, 'bk': jnp.zeros((D,), jnp.float32), 'Wv': jax.random.normal(ks[5], (D, D), jnp.float32) * scale, 'bv': jnp.zeros((D,), jnp.float32), 'Wo': jax.random.normal(ks[6], (D, D), jnp.float32) * scale, 'bo': jnp.zeros((D,), jnp.float32)}
        return inp
    _L0_xattn_all = _L0_xattn_setup()
    _L0_xattn_in = {k: v for k, v in _L0_xattn_all.items() if k in ('Wq', 'bq', 'Wk', 'bk', 'Wv', 'bv', 'Wo', 'bo')}
    del _L0_xattn_all

    def _L0_ffn_setup():
        import jax, jax.numpy as jnp
        import numpy as np
        E = 32
        K = 4
        H = 128
        I = 96
        ROUTED_SCALING_FACTOR = 1.0
        key = jax.random.key(seed)
        k0, k1, k2, k3, k4, k5 = jax.random.split(key, 6)
        return {'hidden_states': jax.random.normal(k0, (1, 256, H), jnp.float32), 'gate_w': jax.random.normal(k1, (E, H), jnp.float32) * 0.02, 'w1': jax.random.normal(k2, (E, H, I), jnp.float32) * 0.02, 'w3': jax.random.normal(k3, (E, H, I), jnp.float32) * 0.02, 'w2': jax.random.normal(k4, (E, I, H), jnp.float32) * 0.02, 'e_bias': jax.random.normal(k5, (E,), jnp.float32) * 0.02}
    _L0_ffn_all = _L0_ffn_setup()
    _L0_ffn_in = {k: v for k, v in _L0_ffn_all.items() if k in ('gate_w', 'w1', 'w3', 'w2', 'e_bias')}
    del _L0_ffn_all

    def _L1_xattn_setup():
        import jax, jax.numpy as jnp
        import numpy as np
        B, S, D = (2, 256, 128)
        H, HD = (16, 64)
        key = jax.random.key(seed)
        ks = jax.random.split(key, 10)
        inp = {'queries': jax.random.normal(ks[0], (B, S, D), jnp.float32), 'keys': jax.random.normal(ks[1], (B, S, D), jnp.float32), 'values': jax.random.normal(ks[2], (B, S, D), jnp.float32), 'ind_q': (jax.random.uniform(ks[3], (B, S)) > 0.2).astype(jnp.float32), 'ind_k': (jax.random.uniform(ks[4], (B, S)) > 0.2).astype(jnp.float32), 'ind_v': (jax.random.uniform(ks[5], (B, S)) > 0.2).astype(jnp.float32), 'Wq': jax.random.normal(ks[6], (D, H * HD), jnp.float32) / np.sqrt(D), 'Wk': jax.random.normal(ks[7], (D, H * HD), jnp.float32) / np.sqrt(D), 'Wv': jax.random.normal(ks[8], (D, H * HD), jnp.float32) / np.sqrt(D), 'Wo': jax.random.normal(ks[9], (H * HD, D), jnp.float32) / np.sqrt(H * HD)}
        return inp
    _L1_xattn_all = _L1_xattn_setup()
    _L1_xattn_in = {k: v for k, v in _L1_xattn_all.items() if k in ('Wq', 'Wk', 'Wv', 'Wo')}
    del _L1_xattn_all

    def _L1_ffn_setup():
        import jax, jax.numpy as jnp
        import numpy as np
        B, S, D = (1, 256, 128)
        E, K, H = (8, 2, 64)
        HS = 128
        key = jax.random.key(seed)
        ks = jax.random.split(key, 8)
        sc = lambda fan_in: 1.0 / np.sqrt(fan_in)
        return {'x': jax.random.normal(ks[0], (B, S, D), jnp.float32), 'gate_w': jax.random.normal(ks[1], (D, E), jnp.float32) * sc(D), 'w1': jax.random.normal(ks[2], (E, D, H), jnp.float32) * sc(D), 'w3': jax.random.normal(ks[3], (E, D, H), jnp.float32) * sc(D), 'w2': jax.random.normal(ks[4], (E, H, D), jnp.float32) * sc(H), 'ws1': jax.random.normal(ks[5], (D, HS), jnp.float32) * sc(D), 'ws3': jax.random.normal(ks[6], (D, HS), jnp.float32) * sc(D), 'ws2': jax.random.normal(ks[7], (HS, D), jnp.float32) * sc(HS)}
    _L1_ffn_all = _L1_ffn_setup()
    _L1_ffn_in = {k: v for k, v in _L1_ffn_all.items() if k in ('gate_w', 'w1', 'w3', 'w2', 'ws1', 'ws3', 'ws2')}
    del _L1_ffn_all
    return {'x': x, 'ctx_1024': ctx_1024, 'mask_BxS2_fk1': mask_BxS2_fk1, 'L0_xattn_Wq': _L0_xattn_in['Wq'], 'L0_xattn_bq': _L0_xattn_in['bq'], 'L0_xattn_Wk': _L0_xattn_in['Wk'], 'L0_xattn_bk': _L0_xattn_in['bk'], 'L0_xattn_Wv': _L0_xattn_in['Wv'], 'L0_xattn_bv': _L0_xattn_in['bv'], 'L0_xattn_Wo': _L0_xattn_in['Wo'], 'L0_xattn_bo': _L0_xattn_in['bo'], 'L0_ffn_gate_w': _L0_ffn_in['gate_w'], 'L0_ffn_w1': _L0_ffn_in['w1'], 'L0_ffn_w3': _L0_ffn_in['w3'], 'L0_ffn_w2': _L0_ffn_in['w2'], 'L0_ffn_e_bias': _L0_ffn_in['e_bias'], 'L1_xattn_Wq': _L1_xattn_in['Wq'], 'L1_xattn_Wk': _L1_xattn_in['Wk'], 'L1_xattn_Wv': _L1_xattn_in['Wv'], 'L1_xattn_Wo': _L1_xattn_in['Wo'], 'L1_ffn_gate_w': _L1_ffn_in['gate_w'], 'L1_ffn_w1': _L1_ffn_in['w1'], 'L1_ffn_w3': _L1_ffn_in['w3'], 'L1_ffn_w2': _L1_ffn_in['w2'], 'L1_ffn_ws1': _L1_ffn_in['ws1'], 'L1_ffn_ws3': _L1_ffn_in['ws3'], 'L1_ffn_ws2': _L1_ffn_in['ws2']}

def reference(x, ctx_1024, mask_BxS2_fk1, L0_xattn_Wq, L0_xattn_bq, L0_xattn_Wk, L0_xattn_bk, L0_xattn_Wv, L0_xattn_bv, L0_xattn_Wo, L0_xattn_bo, L0_ffn_gate_w, L0_ffn_w1, L0_ffn_w3, L0_ffn_w2, L0_ffn_e_bias, L1_xattn_Wq, L1_xattn_Wk, L1_xattn_Wv, L1_xattn_Wo, L1_ffn_gate_w, L1_ffn_w1, L1_ffn_w3, L1_ffn_w2, L1_ffn_ws1, L1_ffn_ws3, L1_ffn_ws2):
    import jax
    import jax.numpy as jnp

    def _L0_xattn_ref(q, k, v, Wq, bq, Wk, bk, Wv, bv, Wo, bo):
        import jax, jax.numpy as jnp
        import numpy as np
        D_MODEL = 128
        NHEAD = 16
        HEAD_DIM = D_MODEL // NHEAD
        B, S, D = q.shape
        H, Hd = (NHEAD, HEAD_DIM)
        qh = (q @ Wq.T + bq).reshape(B, S, H, Hd).transpose(0, 2, 1, 3)
        kh = (k @ Wk.T + bk).reshape(B, S, H, Hd).transpose(0, 2, 1, 3)
        vh = (v @ Wv.T + bv).reshape(B, S, H, Hd).transpose(0, 2, 1, 3)
        scores = jnp.einsum('bhqd,bhkd->bhqk', qh, kh) / jnp.sqrt(jnp.float32(Hd))
        attn = jax.nn.softmax(scores, axis=-1)
        out = jnp.einsum('bhqk,bhkd->bhqd', attn, vh)
        out = out.transpose(0, 2, 1, 3).reshape(B, S, D)
        return out @ Wo.T + bo

    def _L0_ffn_ref(hidden_states, gate_w, w1, w3, w2, e_bias):
        import jax, jax.numpy as jnp
        import numpy as np
        E = 32
        K = 4
        H = 128
        I = 96
        ROUTED_SCALING_FACTOR = 1.0
        orig_shape = hidden_states.shape
        x = hidden_states.reshape(-1, orig_shape[-1])
        T = x.shape[0]
        router_logits = x @ gate_w.T
        scores = jax.nn.sigmoid(router_logits.astype(jnp.float32))
        _, topk_ids = jax.lax.top_k(scores + e_bias[None, :], K)
        topk_w = jnp.take_along_axis(scores, topk_ids, axis=1)
        topk_w = topk_w / jnp.sum(topk_w, axis=1, keepdims=True)
        combine = jnp.zeros((T, E), jnp.float32).at[jnp.arange(T)[:, None], topk_ids].add(topk_w)
        g = jnp.einsum('th,ehi->tei', x, w1)
        u = jnp.einsum('th,ehi->tei', x, w3)
        a = jax.nn.silu(g) * u * combine[:, :, None].astype(x.dtype)
        out = jnp.einsum('tei,eih->th', a, w2)
        out = out * ROUTED_SCALING_FACTOR
        return out.reshape(orig_shape)

    def _L1_xattn_ref(queries, keys, values, ind_q, ind_k, ind_v, Wq, Wk, Wv, Wo):
        import jax, jax.numpy as jnp
        import numpy as np
        B, S, D = (2, 256, 128)
        H, HD = (16, 64)
        b, nq, _ = queries.shape
        nk = keys.shape[1]
        Q = (queries @ Wq).reshape(b, nq, H, HD).transpose(0, 2, 1, 3) * ind_q[:, None, :, None]
        K = (keys @ Wk).reshape(b, nk, H, HD).transpose(0, 2, 1, 3) * ind_k[:, None, :, None]
        V = (values @ Wv).reshape(b, nk, H, HD).transpose(0, 2, 1, 3) * ind_v[:, None, :, None]
        scores = jnp.einsum('bhqd,bhkd->bhqk', Q, K) / jnp.sqrt(jnp.float32(HD))
        attn = jax.nn.softmax(scores, axis=-1)
        attn = attn * ind_k[:, None, None, :]
        denom = jnp.sum(attn, axis=-1, keepdims=True)
        attn = attn / jnp.where(denom == 0.0, 1.0, denom)
        out = jnp.einsum('bhqk,bhkd->bhqd', attn, V)
        out = out.transpose(0, 2, 1, 3).reshape(b, nq, H * HD)
        return out @ Wo

    def _L1_ffn_ref(x, gate_w, w1, w3, w2, ws1, ws3, ws2):
        import jax, jax.numpy as jnp
        import numpy as np
        B, S, D = (1, 256, 128)
        E, K, H = (8, 2, 64)
        HS = 128
        b, s, d = x.shape
        xt = x.reshape(-1, d)
        T = xt.shape[0]
        scores = jax.nn.sigmoid(xt @ gate_w)
        top_scores, top_idx = jax.lax.top_k(scores, K)
        top_scores = top_scores / jnp.sum(top_scores, axis=-1, keepdims=True)
        dense = jnp.zeros((T, E), xt.dtype).at[jnp.arange(T)[:, None], top_idx].set(top_scores)
        h = jax.nn.silu(jnp.einsum('td,edh->teh', xt, w1)) * jnp.einsum('td,edh->teh', xt, w3)
        y = jnp.einsum('teh,ehd->ted', h, w2)
        routed = jnp.einsum('ted,te->td', y, dense)
        shared = jax.nn.silu(xt @ ws1) * (xt @ ws3) @ ws2
        return (shared + routed).reshape(b, s, d)
    x = x + _L0_xattn_ref(_layernorm(x, axis=-1), ctx_1024, ctx_1024, L0_xattn_Wq, L0_xattn_bq, L0_xattn_Wk, L0_xattn_bk, L0_xattn_Wv, L0_xattn_bv, L0_xattn_Wo, L0_xattn_bo)
    x = x + _L0_ffn_ref(_layernorm(x, axis=-1), L0_ffn_gate_w, L0_ffn_w1, L0_ffn_w3, L0_ffn_w2, L0_ffn_e_bias)
    x = x + _L1_xattn_ref(_layernorm(x, axis=-1), ctx_1024, ctx_1024, mask_BxS2_fk1, mask_BxS2_fk1, mask_BxS2_fk1, L1_xattn_Wq, L1_xattn_Wk, L1_xattn_Wv, L1_xattn_Wo)
    x = x + _L1_ffn_ref(_layernorm(x, axis=-1), L1_ffn_gate_w, L1_ffn_w1, L1_ffn_w3, L1_ffn_w2, L1_ffn_ws1, L1_ffn_ws3, L1_ffn_ws2)
    return x

_drawn_inputs = setup_inputs


def setup_inputs(seed=0):
    import zlib

    import numpy as np

    out = dict(_drawn_inputs(seed))
    spreads = {'L0_xattn_bq': (0.0, 0.1),
     'L0_xattn_bk': (0.0, 0.8),
     'L0_xattn_bv': (0.0, 0.1),
     'L0_xattn_bo': (0.0, 0.1)}
    factors = {'L0_ffn_gate_w': 6.407,
     'L0_ffn_w1': 5.309,
     'L0_ffn_w3': 5.659,
     'L0_ffn_w2': 5.843,
     'L0_ffn_e_bias': 7.376}
    for name, (base, spread) in spreads.items():
        noise = np.random.default_rng([zlib.crc32(name.encode()), seed]).standard_normal(out[name].shape)
        drawn = base * np.exp(spread * noise) if base else spread * noise
        out[name] = jnp.asarray(drawn.astype(out[name].dtype))
    for name, factor in factors.items():
        out[name] = (out[name] * factor).astype(out[name].dtype)
    return out
```

```python
import concourse.bass as bass
from concourse import mybir
from contextlib import ExitStack

import numpy as np

F32 = mybir.dt.float32
F32R = mybir.dt.float32r
ACT = mybir.ActivationFunctionType
ALU = mybir.AluOpType
AX = mybir.AxisListType

B, S, D = 32, 128, 128
P = 128
H = 16
D0, D1 = D // H, 64
GB = 4
G = B // GB
NU = 4
US = GB * NU
LEAD = 5
EPS = 1e-5
E0, I0, K0 = 32, 96, 4
E1, I1, K1, HS = 8, 64, 2, 128
TINY = 1e-37
NONE = -1e30


class Attn:

    def __init__(self, layer):
        self.layer = layer
        if layer == 0:
            self.rows, self.hd, self.nchunk, self.nsel = 32, D0, 4, 4
            self.scale = float(np.float32(1.0) / np.sqrt(np.float32(D0)))
        else:
            self.rows, self.hd, self.nchunk, self.nsel = 64, D1, 8, 8
            self.scale = float(np.float32(1.0) / np.sqrt(np.float32(D1)))
        self.npart = P // self.rows
        self.nqk = self.nchunk // 4
        self.nv = H * self.hd // 512 if layer else 1
        self.fills = 1 + 2 * self.nqk + self.nv
        self.natt = H * self.hd // 512 if layer else 1
        self.fill_rows = [[0], [1], [2], [3]] if layer == 0 else [[0], [1, 2], [3, 4], [5, 6]]

    def unit(self, r):
        part = r if self.layer == 0 else r // 2
        first = 0 if self.layer == 0 else 4 * (r % 2)
        return [(first + i, part * self.rows, (first + i) * self.npart + part) for i in range(4)]


def attention(nc, mem, layer, bank, x_all, ctx_all, const, weights):
    c = Attn(layer)
    RW, NQ, NV, NF, HD = c.rows, c.nqk, c.nv, c.fills, c.hd
    ctx = mem

    def sb(name, shape, dt=F32):
        return ctx.enter_context(nc.sbuf_tensor(f"{name}_l{layer}", shape, dt))

    def sem(name):
        return ctx.enter_context(nc.semaphore(f"{name}_l{layer}"))

    ident = const["ident"]
    xhat = sb("xhat", [P, 2, D])
    ctxm = sb("ctxm", [P, 2, D])
    stats = sb("stats", [P, 2, 6])
    meanvar = sb("meanvar", [P, 2, 2])
    vareps = sb("vareps", [P, 2, 1])
    deviation_inv = sb("deviation_inv", [P, 2, 1]) if layer else None
    rstd = sb("rstd", [P, 2, 1])
    xc_hi = sb("xc_hi", [P, 2 * P], F32R)
    xc_lo = sb("xc_lo", [P, 2 * P], F32R)
    q_a = sb("q_a", [P, 4, c.nchunk, P], F32R)
    k_a = sb("k_a", [P, 4, c.nchunk, P], F32R)
    if layer:
        q_b = sb("q_b", [P, 4, c.nchunk, P], F32R)
        k_b = sb("k_b", [P, 4, c.nchunk, P], F32R)
    part_q = sb("part_q", [P, 2, 512], F32R) if layer == 0 else None
    v = sb("v", [P, 4, H, HD + 1])
    negmax = sb("negmax", [P, 2, P])
    negmax_t = sb("negmax_t", [P, 2, P], F32R)
    probs = sb("probs", [P, 2, 512])
    rden = sb("rden", [P, 2, 4])
    den = sb("den", [P, 2, 4])
    att = sb("att", [P, 2, H * HD])
    att_t = sb("att_t", [P, 2, c.natt * 512 if layer else P])

    M_BANK, T_BANK, PV_BANK, TR_BANK, PJ_BANK = [0, 1], [2, 3], 4, 5, [6, 7]

    s_stats, s_mv, s_var, s_rstd, s_xhat, s_xpre = (sem(n) for n in ("stats", "mv", "var", "rstd", "xhat", "xpre"))
    s_fill, s_upper, s_lower = sem("fill"), sem("upper"), sem("lower")
    s_max_mm, s_max = sem("max_mm"), sem("max")
    s_nmt_mm, s_nmt = sem("nmt_mm"), sem("nmt")
    s_scores, s_exp, s_pv, s_rden, s_att = sem("scores"), sem("exp"), sem("pv"), sem("rden"), sem("att")
    s_att_mm, s_att_t, s_out_mm, s_x = sem("att_mm"), sem("att_t"), sem("out_mm"), sem("x")
    s_zero = sem("zero")
    s_den = sem("den")
    s_vcol = sem("vcol")
    s_apart = sem("apart")

    def tile(t, b):
        return t[:, bass.ds(b * D, D)]

    def schedule(body, loop, prologue, tail):
        prologue()
        body(0, first=True, last=False)
        with loop(1, G - 1) as g:
            body(g, first=False, last=False)
        body(G - 1, first=False, last=True)
        tail()

    with nc.Block() as block:

        @block.tensor
        def _(pe):
            def fill(b, i, ring, parity):
                bank_ = bank[PJ_BANK[(parity * NF + i) % 2]]
                if i == 0:
                    pe.wait_ge(s_xhat, b + 1)
                    pe.wait_ge(s_xpre, b + 1)
                if not (isinstance(b, int) and b * NF + i < 2):
                    pe.wait_ge(s_lower, b * NF + i - 1)
                if i == 0:
                    nc.tensor.transpose(bank_[:, 0:P], xhat[:, parity, :], ident[:])
                    nc.tensor.transpose(bank_[:, P:2 * P], ctxm[:, parity, :], ident[:]).then_inc(s_fill, 1)
                    return
                if i == 1:
                    pe.wait_ge(s_lower, b * NF + 1)
                x_hi, x_lo = xc_hi[:, 0:P], xc_lo[:, 0:P]
                c_hi, c_lo = xc_hi[:, P:2 * P], xc_lo[:, P:2 * P]
                if i <= 2 * NQ:
                    isq = i <= NQ
                    w_hi, w_lo = weights["wq" if isq else "wk"]
                    m_hi, m_lo = (x_hi, x_lo) if isq else (c_hi, c_lo)
                    j0 = 4 * ((i - 1) % NQ)
                    for j in range(4):
                        cols = slice((j0 + j) * P, (j0 + j + 1) * P)
                        o = bank_[:, j * P:(j + 1) * P]
                        nc.tensor.matmul(o, w_hi[:, cols], m_hi, start=True, stop=False)
                        nc.tensor.matmul(o, w_hi[:, cols], m_lo, start=False, stop=False)
                        last_ = nc.tensor.matmul(o, w_lo[:, cols], m_hi, start=False, stop=True)
                else:
                    n = i - 1 - 2 * NQ
                    w_hi, w_lo = weights["wv"]
                    width = 512 if layer else D
                    cols = slice(n * width, (n + 1) * width)
                    o = bank_[:, 0:width]
                    nc.tensor.matmul(o, c_hi, w_hi[:, cols], start=True, stop=False)
                    nc.tensor.matmul(o, c_hi, w_lo[:, cols], start=False, stop=False)
                    last_ = nc.tensor.matmul(o, c_lo, w_hi[:, cols], start=False, stop=True)
                last_.then_inc(s_fill, 1)

            def maxima(u, b, ring, r, slot, wait):
                if r == 0:
                    pe.wait_ge(s_lower, b * NF + 1 + 2 * NQ)
                if wait:
                    pe.wait_ge(s_max, u - 1)
                for i, (ch, row, _) in enumerate(c.unit(r)):
                    last_ = nc.tensor.matmul(bank[M_BANK[slot % 2]][:, i * P:(i + 1) * P],
                                             q_a[row:row + RW, ring, ch, :], k_a[row:row + RW, ring, ch, :],
                                             start=True, stop=True)
                last_.then_inc(s_max_mm, 1)

            def transpose_maxima(b, parity, wait):
                pe.wait_ge(s_max, NU * b + NU)
                if wait:
                    pe.wait_ge(s_x, b - 1)
                nc.tensor.transpose(bank[TR_BANK][:, 0:P], negmax[:, parity, :], ident[:]).then_inc(s_nmt_mm, 1)

            def scores(u, b, ring, parity, r, wait):
                if r == 0:
                    pe.wait_ge(s_nmt, b + 1)
                if wait:
                    pe.wait_ge(s_exp, u - 1)
                for i, (ch, row, _) in enumerate(c.unit(r)):
                    rows = slice(row, row + RW)
                    o = bank[T_BANK[r % 2]][:, i * P:(i + 1) * P]
                    if layer == 0:
                        nc.tensor.matmul(o, k_a[rows, ring, ch, :], q_a[rows, ring, ch, :], start=True, stop=False)
                    else:
                        nc.tensor.matmul(o, k_a[rows, ring, ch, :], q_a[rows, ring, ch, :], start=True, stop=False)
                        nc.tensor.matmul(o, k_a[rows, ring, ch, :], q_b[rows, ring, ch, :], start=False, stop=False)
                        nc.tensor.matmul(o, k_b[rows, ring, ch, :], q_a[rows, ring, ch, :], start=False, stop=False)
                    sel = const["sel"][rows, (i if layer == 0 else ch), :]
                    last_ = nc.tensor.matmul(o, sel, negmax_t[rows, parity, :], start=False, stop=True)
                last_.then_inc(s_scores, 1)

            def values(u, b, ring, r, wait):
                if r == 0:
                    pe.wait_ge(s_lower, NF * b + NF)
                    if layer:
                        pe.wait_ge(s_vcol, b + 1)
                pe.wait_ge(s_exp, u + 1)
                if wait:
                    pe.wait_ge(s_att, u)
                for i, (_, _, h) in enumerate(c.unit(r)):
                    last_ = nc.tensor.matmul(bank[PV_BANK][:, i * (HD + 1):(i + 1) * (HD + 1)],
                                             probs[:, r % 2, i * P:(i + 1) * P], v[:, ring, h, :],
                                             start=True, stop=True)
                last_.then_inc(s_pv, 1)

            def transpose_att(b, parity, n):
                pe.wait_ge(s_att, NU * b + NU)
                if n:
                    pe.wait_ge(s_att_t, b * c.natt + n)
                width = min(4, c.natt * 4 if layer else 1)
                for j in range(width):
                    last_ = nc.tensor.transpose(bank[TR_BANK][:, j * P:(j + 1) * P],
                                                att[:, parity, (4 * n + j) * P:(4 * n + j + 1) * P], ident[:])
                last_.then_inc(s_att_mm, 1)

            def out(b, parity):
                pe.wait_ge(s_att_t, b * c.natt + c.natt)
                n = H * HD // P
                for j in range(n):
                    last_ = nc.tensor.matmul(bank[TR_BANK][:, 0:D], att_t[:, parity, j * P:(j + 1) * P],
                                             weights["wo"][:, j, :], start=(j == 0), stop=(j == n - 1))
                last_.then_inc(s_out_mm, 1)

            def prologue():
                for b in range(2):
                    for i in range(NF):
                        fill(b, i, b, b % 2)
                for u in range(LEAD):
                    maxima(u, u // NU, u // NU, u % NU, u, wait=u >= 2)
                transpose_maxima(0, 0, wait=False)

            def body(g, first, last):
                for s in range(US):
                    j, r = divmod(s, NU)
                    b, u = g * GB + j, g * US + s
                    static = isinstance(g, int)
                    prev = not (first and j == 0)
                    scores(u, b, j, j % 2, r, wait=not (static and g == 0 and s < 2))
                    if not (first and s == 0):
                        pj, pr = (j, r - 1) if r else ((j - 1) % GB, NU - 1)
                        values(u - 1, (b if r else b - 1), pj, pr, wait=not (first and s == 1))
                    if r == 1 and prev:
                        transpose_att(b - 1, (j - 1) % 2, 0)
                    if not (last and j >= 2):
                        for i in c.fill_rows[r]:
                            fill(b + 2, i, (j + 2) % GB, j % 2)
                    if not (last and s + LEAD >= US):
                        t = s + LEAD
                        maxima(u + LEAD, b + (r + LEAD) // NU, (t // NU) % GB, t % NU, t, wait=True)
                    if r == 1 and prev and c.natt == 2:
                        transpose_att(b - 1, (j - 1) % 2, 1)
                    if r == 2 and prev:
                        out(b - 1, (j - 1) % 2)
                    if r == NU - 1 and not (last and j == GB - 1):
                        transpose_maxima(b + 1, (j + 1) % 2, wait=not (static and b < 1))

            def tail():
                values(B * NU - 1, B - 1, GB - 1, NU - 1, wait=True)
                for n in range(c.natt):
                    transpose_att(B - 1, 1, n)
                out(B - 1, 1)

            schedule(body, pe.Fori, prologue, tail)

        @block.scalar
        def _(act):
            def fill(b, i, ring, parity):
                bank_ = bank[PJ_BANK[(parity * NF + i) % 2]]
                act.wait_ge(s_fill, b * NF + i + 1)
                if i == 0:
                    nc.scalar.activation(xc_hi[:, :], bank_[:, 0:2 * P], ACT.Copy).then_inc(s_upper, 1)
                elif i <= 2 * NQ:
                    isq = i <= NQ
                    if layer == 0:
                        m, mb = (0, 0) if isq else (1, 1)
                        for ch in range(4):
                            last_ = nc.scalar.activation(part_q[:, i % 2, ch * P:(ch + 1) * P],
                                                         bank_[:, ch * P:(ch + 1) * P], ACT.Identity,
                                                         scale=const["low"][:, m:m + 1],
                                                         bias=weights["low_bias"][:, 4 * mb + ch:4 * mb + ch + 1])
                        last_.then_inc(s_upper, 1)
                    else:
                        j0 = 4 * ((i - 1) % NQ)
                        dst = (q_a if isq else k_a)[:, ring, j0:j0 + 4, :]
                        nc.scalar.activation(dst, bank_[:, :].rearrange("p (a b) -> p a b", b=P),
                                             ACT.Copy).then_inc(s_upper, 1)

            def transposed_maxima(b, parity):
                act.wait_ge(s_nmt_mm, b + 1)
                nc.scalar.activation(negmax_t[:, parity, :], bank[TR_BANK][:, 0:P], ACT.Copy).then_inc(s_nmt, 1)

            def exponentials(u, r, wait):
                act.wait_ge(s_scores, u + 1)
                if wait:
                    act.wait_ge(s_pv, u - 1)
                nc.scalar.activation(probs[:, r % 2, :], bank[T_BANK[r % 2]][:, :], ACT.Exp,
                                     scale=c.scale).then_inc(s_exp, 1)

            def transposed_att(b, parity, n):
                act.wait_ge(s_att_mm, b * c.natt + n + 1)
                width = 512 if layer else P
                nc.scalar.activation(att_t[:, parity, n * 512:n * 512 + width], bank[TR_BANK][:, 0:width],
                                     ACT.Copy).then_inc(s_att_t, 1)

            def prologue():
                for b in range(2):
                    for i in range(1 + 2 * NQ):
                        fill(b, i, b, b % 2)
                transposed_maxima(0, 0)

            def body(g, first, last):
                for s in range(US):
                    j, r = divmod(s, NU)
                    b, u = g * GB + j, g * US + s
                    prev = not (first and j == 0)
                    exponentials(u, r, wait=not (first and s < 2))
                    if r == 1 and prev:
                        transposed_att(b - 1, (j - 1) % 2, 0)
                    if not (last and j >= 2):
                        for i in c.fill_rows[r]:
                            fill(b + 2, i, (j + 2) % GB, j % 2)
                    if r == 1 and prev and c.natt == 2:
                        transposed_att(b - 1, (j - 1) % 2, 1)
                    if r == NU - 1 and not (last and j == GB - 1):
                        transposed_maxima(b + 1, (j + 1) % 2)

            def tail():
                for n in range(c.natt):
                    transposed_att(B - 1, 1, n)

            schedule(body, act.Fori, prologue, tail)

        @block.vector
        def _(dve):
            def statistics(b, parity):
                nc.vector.bn_stats(stats[:, parity, :], tile(x_all, b)).then_inc(s_stats, 1)
                dve.wait_ge(s_stats, b + 1)
                dve.sem_inc(s_apart, 1)
                nc.vector.bn_aggr(meanvar[:, parity, :], stats[:, parity, :]).then_inc(s_mv, 1)

            def normalise(b, parity):
                dve.wait_ge(s_rstd, b + 1)
                nc.vector.tensor_scalar(xhat[:, parity, :], tile(x_all, b), meanvar[:, parity, 0:1],
                                        rstd[:, parity, :], ALU.subtract, ALU.mult).then_inc(s_xhat, 1)

            def fill(b, i, ring, parity):
                bank_ = bank[PJ_BANK[(parity * NF + i) % 2]]
                if i <= 2 * NQ:
                    dve.wait_ge(s_upper, b * (1 + 2 * NQ) + i + 1)
                if i == 0:
                    nc.vector.tensor_tensor(xc_lo[:, :], bank_[:, 0:2 * P], xc_hi[:, :].bitcast(F32),
                                            ALU.subtract).then_inc(s_lower, 1)
                elif i <= 2 * NQ:
                    isq = i <= NQ
                    if layer == 0:
                        m = 0 if isq else 4
                        dst = (q_a if isq else k_a)
                        for ch in range(4):
                            last_ = nc.vector.scalar_tensor_tensor(
                                dst[:, ring, ch, :], bank_[:, ch * P:(ch + 1) * P],
                                weights["bias"][:, m + ch:m + ch + 1],
                                part_q[:, i % 2, ch * P:(ch + 1) * P].bitcast(F32), ALU.add, ALU.subtract)
                        last_.then_inc(s_lower, 1)
                    else:
                        j0 = 4 * ((i - 1) % NQ)
                        up, lo = (q_a, q_b) if isq else (k_a, k_b)
                        nc.vector.tensor_tensor(lo[:, ring, j0:j0 + 4, :],
                                                bank_[:, :].rearrange("p (a b) -> p a b", b=P),
                                                up[:, ring, j0:j0 + 4, :].bitcast(F32),
                                                ALU.subtract).then_inc(s_lower, 1)
                else:
                    n = i - 1 - 2 * NQ
                    dve.wait_ge(s_fill, b * NF + i + 1)
                    nh = 512 // HD if layer else H
                    src = bank_[:, 0:nh * HD].rearrange("p (h d) -> p h d", d=HD)
                    dst = v[:, ring, n * nh:(n + 1) * nh, 0:HD]
                    if layer == 0:
                        nc.vector.tensor_tensor(dst, src, weights["bv"][:, :].rearrange("p (h d) -> p h d", d=HD),
                                                ALU.add).then_inc(s_lower, 1)
                    else:
                        nc.vector.tensor_scalar(dst, src, const["mask"][:, bass.ds(b, 1)], None,
                                                ALU.mult).then_inc(s_lower, 1)

            def maxima(u, r, slot, parity):
                dve.wait_ge(s_max_mm, u + 1)
                m0 = c.unit(r)[0][1] + (0 if layer == 0 else c.unit(r)[0][0])
                nc.vector.tensor_reduce(negmax[:, parity, m0:m0 + 4],
                                        bank[M_BANK[slot % 2]][:, :].rearrange("p (a b) -> p a b", b=P),
                                        AX.X, ALU.max, negate=True).then_inc(s_max, 1)

            def attention_out(u, r, parity):
                dve.wait_ge(s_pv, u + 1)
                o = bank[PV_BANK][:, 0:4 * (HD + 1)].rearrange("p (a b) -> p a b", b=HD + 1)
                nc.vector.tensor_scalar(den[:, r % 2, :], o[:, :, HD], TINY, None, ALU.max).then_inc(s_den, 1)
                dve.wait_ge(s_den, u + 1)
                nc.vector.reciprocal(rden[:, r % 2, :], den[:, r % 2, :]).then_inc(s_rden, 1)
                dve.wait_ge(s_rden, u + 1)
                h0 = c.unit(r)[0][2]
                dst = att[:, parity, :].rearrange("p (c n d) -> p c n d", n=c.npart, d=HD)
                dst = dst[:, h0 // c.npart:h0 // c.npart + 4, h0 % c.npart, :]
                nc.vector.tensor_tensor(dst, o[:, :, 0:HD],
                                        rden[:, r % 2, :].unsqueeze(2).broadcast_to([P, 4, HD]),
                                        ALU.mult).then_inc(s_att, 1)

            def add(b):
                dve.wait_ge(s_out_mm, b + 1)
                if layer == 0:
                    dve.wait_ge(s_xpre, b + 1)
                nc.vector.tensor_tensor(tile(x_all, b), bank[TR_BANK][:, 0:D], tile(x_all, b),
                                        ALU.add).then_inc(s_x, 1)

            def prologue():
                nc.vector.memset(negmax[:, :, :], 0.0).then_inc(s_zero, 1)
                if layer == 0:
                    nc.vector.memset(v[:, :, :, HD], 1.0).then_inc(s_zero, 1)
                dve.wait_ge(s_zero, 1 + (layer == 0))
                for b in range(3):
                    if b == 2:
                        for n in range(2):
                            for i in range(NF):
                                fill(n, i, n, n % 2)
                    statistics(b, b % 2)
                    normalise(b, b % 2)
                for u in range(LEAD):
                    maxima(u, u % NU, u, (u // NU) % 2)

            def body(g, first, last):
                for s in range(US):
                    j, r = divmod(s, NU)
                    b, u = g * GB + j, g * US + s
                    prev = not (first and j == 0)
                    if not (first and s == 0):
                        pj, pr = (j, r - 1) if r else ((j - 1) % GB, NU - 1)
                        attention_out(u - 1, pr, pj % 2)
                    if not (last and j >= 2):
                        for i in c.fill_rows[r]:
                            fill(b + 2, i, (j + 2) % GB, j % 2)
                    if not (last and s + LEAD >= US):
                        t = s + LEAD
                        maxima(u + LEAD, t % NU, t, (t // NU) % 2)
                    if r == 1 and not (last and j >= 1):
                        statistics(b + 3, (j + 3) % 2)
                    if r == 3 and not (last and j >= 1):
                        normalise(b + 3, (j + 3) % 2)
                    if r == 2 and prev:
                        add(b - 1)

            def tail():
                attention_out(B * NU - 1, NU - 1, 1)
                add(B - 1)

            schedule(body, dve.Fori, prologue, tail)

        @block.gpsimd
        def _(pool):
            def deviation(b, parity):
                pool.wait_ge(s_mv, b + 1)
                nc.gpsimd.tensor_tensor(vareps[:, parity, :], meanvar[:, parity, 1:2], const["eps"][:, :],
                                        ALU.add).then_inc(s_var, 1)
                pool.wait_ge(s_var, (2 if layer else 1) * b + 1)
                nc.gpsimd.tensor_tensor(rstd[:, parity, :] if not layer else deviation_inv[:, parity, :],
                                        vareps[:, parity, :], const["power"][:, :],
                                        ALU.pow).then_inc(s_rstd if not layer else s_var, 1)
                pool.wait_ge(const["s_power"], 1)
                if layer:
                    pool.wait_ge(s_var, 2 * b + 2)
                    nc.gpsimd.tensor_tensor(rstd[:, parity, :], deviation_inv[:, parity, :],
                                            const["mask"][:, bass.ds(b, 1)], ALU.mult).then_inc(s_rstd, 1)

            def context(b, ring, parity, wait, used):
                pool.wait_ge(const["s_power"], 1)
                if wait:
                    pool.wait_ge(s_fill, (b - 2) * NF + 1)
                if layer:
                    nc.gpsimd.tensor_tensor(ctxm[:, parity, :], tile(ctx_all, b),
                                            const["mask"][:, bass.ds(b, 1)].broadcast_to([P, D]),
                                            ALU.mult).then_inc(s_xpre, 1)
                    if used:
                        pool.wait_ge(s_pv, NU * (b - 3))
                        pool.sem_inc(s_apart, 1)
                    nc.gpsimd.tensor_copy(v[:, ring, :, HD],
                                          const["mask"][:, bass.ds(b, 1)].broadcast_to([P, H])).then_inc(s_vcol, 1)
                else:
                    nc.gpsimd.tensor_copy(ctxm[:, parity, :], tile(ctx_all, b))
                    pool.wait_ge(const["s_power"], 1)
                    pool.wait_ge(s_xhat, b + 1)
                    nc.gpsimd.tensor_tensor(tile(x_all, b), tile(x_all, b), weights["bo"][:, :],
                                            ALU.add).then_inc(s_xpre, 1)

            def prologue():
                for b in range(3):
                    deviation(b, b % 2)
                    context(b, b, b % 2, wait=b >= 2, used=False)

            def body(g, first, last):
                for j in range(GB):
                    b = g * GB + j
                    if not (last and j >= 1):
                        deviation(b + 3, (j + 3) % 2)
                        context(b + 3, (j + 3) % GB, (j + 3) % 2, wait=True, used=not (first and j == 0))

            schedule(body, pool.Fori, prologue, lambda: None)


def load_and_split(nc, mem, pairs, plain):
    widest = max(hi.shape[1] for _, hi, _ in pairs)
    stage = [mem.enter_context(nc.sbuf_tensor(f"stage_{nc.next_id()}", [P, widest], F32)) for _ in range(2)]
    s_in = [mem.enter_context(nc.semaphore(f"staged_{nc.next_id()}")) for _ in pairs]
    s_plain = mem.enter_context(nc.semaphore(f"plain_{nc.next_id()}"))
    s_hi = mem.enter_context(nc.semaphore(f"split_upper_{nc.next_id()}"))
    s_lo = mem.enter_context(nc.semaphore(f"split_lower_{nc.next_id()}"))
    with nc.Block() as block:

        @block.sync
        def _(sp):
            for n, (src, hi, _) in enumerate(pairs):
                if n >= 2:
                    sp.wait_ge(s_lo, n - 1)
                sp.dma_start(shaped(stage[n % 2][:, 0:hi.shape[1]], src), src).then_inc(s_in[n], 16)
            for src, dst in plain:
                sp.dma_start(dst, src).then_inc(s_plain, 16)
            sp.wait_ge(s_plain, 16 * len(plain))

        @block.scalar
        def _(act):
            for n, (_, hi, _) in enumerate(pairs):
                act.wait_ge(s_in[n], 16)
                nc.scalar.activation(hi, stage[n % 2][:, 0:hi.shape[1]], ACT.Copy).then_inc(s_hi, 1)

        @block.vector
        def _(dve):
            for n, (_, hi, lo) in enumerate(pairs):
                dve.wait_ge(s_hi, n + 1)
                nc.vector.tensor_tensor(lo, stage[n % 2][:, 0:hi.shape[1]], hi.bitcast(F32),
                                        ALU.subtract).then_inc(s_lo, 1)


def shaped(tile_view, src):
    if len(src.shape) == 2:
        return tile_view
    return tile_view.rearrange("p (a b) -> p a b", b=src.shape[2])


def layer0_weights(nc, mem, bank, const, d, w, raw):
    s_raw, s_mm, s_hi, s_lo, s_lb = (mem.enter_context(nc.semaphore(n)) for n in
                                     ("raw_in", "spread_mm", "spread_hi", "spread_lo", "low_bias_done"))
    with nc.Block() as block:

        @block.sync
        def _(sp):
            for n in ("wq", "wk", "wv", "wo", "gate"):
                sp.dma_start(raw[n][:, :], d[n]).then_inc(s_raw, 16)
            sp.dma_start(raw["b"][:, 0:1], d["bq"]).then_inc(s_raw, 16)
            sp.dma_start(raw["b"][:, 1:2], d["bk"]).then_inc(s_raw, 16)

        @block.tensor
        def _(pe):
            pe.wait_ge(s_raw, 16 * 7)
            nc.tensor.matmul(bank[0][:, :], raw["wq"][:, :], const["expand"][:, :],
                             start=True, stop=True).then_inc(s_mm, 1)
            nc.tensor.matmul(bank[1][:, :], raw["wk"][:, :], const["expand"][:, :],
                             start=True, stop=True).then_inc(s_mm, 1)
            nc.tensor.transpose(bank[2][:, 0:P], raw["wv"][:, :], const["ident"][:]).then_inc(s_mm, 1)
            nc.tensor.transpose(bank[3][:, 0:E0], raw["gate"][:, :], const["ident"][0:E0, 0:E0]).then_inc(s_mm, 1)
            nc.tensor.transpose(bank[4][:, 0:P], raw["wo"][:, :], const["ident"][:]).then_inc(s_mm, 1)
            for n in range(2):
                for ch in range(4):
                    last_ = nc.tensor.matmul(bank[5][:, 4 * n + ch:4 * n + ch + 1],
                                             const["expand"][:, ch * P:(ch + 1) * P], raw["b"][:, n:n + 1],
                                             start=True, stop=True)
            last_.then_inc(s_mm, 1)

        split = [(w["wq"], 512), (w["wk"], 512), (w["wv"], P), (w["gate"], E0)]

        @block.scalar
        def _(act):
            for n, ((hi, _), width) in enumerate(split):
                act.wait_ge(s_mm, n + 1)
                nc.scalar.activation(hi[:, :], bank[n][:, 0:width], ACT.Copy).then_inc(s_hi, 1)
            act.wait_ge(s_mm, 5)
            nc.scalar.activation(w["wo"][:, 0, :], bank[4][:, 0:P], ACT.Copy)

        @block.vector
        def _(dve):
            for n, ((hi, lo), width) in enumerate(split):
                dve.wait_ge(s_hi, n + 1)
                nc.vector.tensor_tensor(lo[:, :], bank[n][:, 0:width], hi[:, :].bitcast(F32),
                                        ALU.subtract).then_inc(s_lo, 1)
            dve.wait_ge(s_mm, 6)
            nc.vector.tensor_copy(w["bias"][:, :], bank[5][:, 0:8]).then_inc(s_lb, 1)
            dve.wait_ge(s_lb, 1)
            for n in range(2):
                nc.vector.tensor_scalar(w["low_bias"][:, 4 * n:4 * n + 4], w["bias"][:, 4 * n:4 * n + 4],
                                        const["low"][:, n:n + 1], None, ALU.mult)


def ffn(nc, mem, layer, bank, x_all, const, w, out):
    ne, width, topk = (E0, I0, K0) if layer == 0 else (E1, I1, K1)
    nc_ = ne * width // P + (0 if layer == 0 else HS // P)
    half = 32 if layer == 0 else 16
    nt = GB
    T = B * S

    def sb(name, shape, dt=F32):
        return mem.enter_context(nc.sbuf_tensor(f"{name}_f{layer}", shape, dt))

    def sem(name):
        return mem.enter_context(nc.semaphore(f"{name}_f{layer}"))

    ident = const["ident"]
    x_hi, x_lo = sb("x_hi", [P, T], F32R), sb("x_lo", [P, T], F32R)
    comb_t = sb("comb_t", [2 * half, T], F32R)
    comb_up = sb("comb_up", [2 * half, 2, 512], F32R)
    xhat = sb("xhat", [P, 2, nt, D])
    stats = sb("stats", [P, 2, nt, 6])
    meanvar = sb("meanvar", [P, 2, nt, 2])
    vareps = sb("vareps", [P, 2, nt])
    rstd = sb("rstd", [P, 2, nt])
    score = sb("score", [P, B, ne])
    biased = sb("biased", [P, B, ne + 4])
    top8 = sb("top8", [P, B, 8])
    top = sb("top", [P, B, 8])
    marked = sb("marked", [P, B, ne + 4])
    total = sb("total", [P, B])
    comb = sb("comb", [P, B, 2 * half])
    gate_act = sb("gate_act", [P, 2, 512])
    hidden = sb("hidden", [P, 2, 512])
    weighted = sb("weighted", [P, 2, 512])
    y_t = sb("y_t", [P, 2, 512])

    s_stats, s_mv, s_var, s_rstd, s_xhat = (sem(n) for n in ("stats", "mv", "var", "rstd", "xhat"))
    s_tr, s_up, s_low, s_route = sem("tr"), sem("up"), sem("low"), sem("route")

    def cols(t, g):
        return t[:, bass.ds(g * 512, 512)]

    def tiles(t, g):
        return t[:, bass.ds(g * nt * D, nt * D)]

    LB = bank[6], bank[7]

    with nc.Block() as block:

        @block.tensor
        def _(pe):
            def logits(g, i):
                pe.wait_ge(s_low, g + 1)
                for t in range(nt):
                    n = g * nt + t
                    o = LB[n * ne // 512][:, n * ne % 512:n * ne % 512 + ne]
                    a = slice(n * P, (n + 1) * P)
                    nc.tensor.matmul(o, x_hi[:, a], w["gate"][0][:, :], start=True, stop=False)
                    nc.tensor.matmul(o, x_hi[:, a], w["gate"][1][:, :], start=False, stop=False)
                    last_ = nc.tensor.matmul(o, x_lo[:, a], w["gate"][0][:, :], start=False, stop=True)
                last_.then_inc(s_route, 1)

            for g in range(G):
                pe.wait_ge(s_xhat, g + 1)
                if g >= 2:
                    pe.wait_ge(s_low, g - 1)
                for t in range(nt):
                    last_ = nc.tensor.transpose(bank[g % 2][:, t * P:(t + 1) * P], xhat[:, g % 2, t, :], ident[:])
                last_.then_inc(s_tr, 1)
                if g >= 1:
                    logits(g - 1, 0)
            logits(G - 1, 0)

        @block.scalar
        def _(act):
            for g in range(G):
                act.wait_ge(s_tr, g + 1)
                nc.scalar.activation(x_hi[:, g * 512:(g + 1) * 512], bank[g % 2][:, :], ACT.Copy).then_inc(s_up, 1)
            act.wait_ge(s_route, G)
            for n in range(0, B * ne, 512):
                m = min(512, B * ne)
                nc.scalar.activation(score[:, n // ne:(n + m) // ne, :],
                                     LB[n // 512][:, 0:m].rearrange("p (a b) -> p a b", b=ne), ACT.Sigmoid)

        @block.vector
        def _(dve):
            def norm(g):
                for t in range(nt):
                    last_ = nc.vector.bn_stats(stats[:, g % 2, t, :], x_all[:, (g * nt + t) * D:(g * nt + t + 1) * D])
                last_.then_inc(s_stats, 1)
                dve.wait_ge(s_stats, g + 1)
                for t in range(nt):
                    last_ = nc.vector.bn_aggr(meanvar[:, g % 2, t, :], stats[:, g % 2, t, :])
                last_.then_inc(s_mv, 1)

            norm(0)
            for g in range(G):
                if g + 1 < G:
                    norm(g + 1)
                dve.wait_ge(s_rstd, g + 1)
                if g >= 2:
                    dve.wait_ge(s_tr, g - 1)
                for t in range(nt):
                    last_ = nc.vector.tensor_scalar(xhat[:, g % 2, t, :],
                                                    x_all[:, (g * nt + t) * D:(g * nt + t + 1) * D],
                                                    meanvar[:, g % 2, t, 0:1], rstd[:, g % 2, t:t + 1],
                                                    ALU.subtract, ALU.mult)
                last_.then_inc(s_xhat, 1)
                dve.wait_ge(s_up, g + 1)
                nc.vector.tensor_tensor(x_lo[:, g * 512:(g + 1) * 512], bank[g % 2][:, :],
                                        x_hi[:, g * 512:(g + 1) * 512].bitcast(F32), ALU.subtract).then_inc(s_low, 1)

        @block.gpsimd
        def _(pool):
            for g in range(G):
                pool.wait_ge(s_mv, g + 1)
                nc.gpsimd.tensor_scalar(vareps[:, g % 2, :], meanvar[:, g % 2, :, 1], EPS, None,
                                        ALU.add).then_inc(s_var, 1)
                pool.wait_ge(s_var, g + 1)
                nc.gpsimd.tensor_tensor(rstd[:, g % 2, :], vareps[:, g % 2, :],
                                        const["power"][:, :].broadcast_to([P, nt]), ALU.pow).then_inc(s_rstd, 1)

    s_c, s_ct, s_cu = sem("choice"), sem("comb_tr"), sem("comb_up")
    s_comb = sem("comb")
    with nc.Block() as block:

        @block.vector
        def _(dve):
            done = [0]

            def after(instruction):
                done[0] += 1
                instruction.then_inc(s_c, 1)
                dve.wait_ge(s_c, done[0])

            nc.vector.memset(biased[:, :, ne:ne + 4], NONE)
            nc.vector.memset(top[:, :, topk:8], NONE)
            if layer == 0:
                after(nc.vector.tensor_tensor(biased[:, :, 0:ne], score[:, :, :],
                                              w["ebias"][:, :].unsqueeze(1).broadcast_to([P, B, ne]), ALU.add))
            else:
                after(nc.vector.tensor_copy(biased[:, :, 0:ne], score[:, :, :]))
                nc.vector.memset(top[:, :, topk:8], NONE)
            for t in range(B):
                last_ = nc.vector.max(top8[:, t, :], biased[:, t, 0:ne])
            after(last_)
            after(nc.vector.tensor_copy(top[:, :, 0:topk], top8[:, :, 0:topk]))
            for t in range(B):
                last_ = nc.vector.match_replace(marked[:, t, :], top[:, t, :], biased[:, t, :], 2.0 * NONE)
            after(last_)
            after(nc.vector.tensor_single_scalar(comb[:, :, 0:ne], marked[:, :, 0:ne], 1.5 * NONE, ALU.is_lt))
            after(nc.vector.tensor_tensor(score[:, :, :], comb[:, :, 0:ne], score[:, :, :], ALU.mult))
            after(nc.vector.tensor_reduce(total[:, :], score[:, :, :], AX.X, ALU.add))
            after(nc.vector.reciprocal(total[:, :], total[:, :]))
            for h in range(2):
                if layer:
                    nc.vector.memset(comb[:, :, h * half + ne:h * half + half], 1.0)
                last_ = nc.vector.tensor_tensor(comb[:, :, h * half:h * half + ne], score[:, :, :],
                                                total[:, :].unsqueeze(2).broadcast_to([P, B, ne]), ALU.mult)
            last_.then_inc(s_comb, 1)
            for g in range(G):
                dve.wait_ge(s_cu, g + 1)
                nc.vector.tensor_tensor(comb_t[:, g * 512:(g + 1) * 512], bank[g % 2][0:2 * half, :],
                                        comb_up[:, g % 2, :].bitcast(F32), ALU.subtract).then_inc(s_ct, 1)

        @block.tensor
        def _(pe):
            pe.wait_ge(s_comb, 1)
            for g in range(G):
                if g >= 2:
                    pe.wait_ge(s_ct, g - 1)
                for t in range(nt):
                    last_ = nc.tensor.transpose(bank[g % 2][0:2 * half, t * P:(t + 1) * P],
                                                comb[:, g * nt + t, :], ident[:])
                last_.then_inc(s_tr, 1)

        @block.scalar
        def _(act):
            for g in range(G):
                act.wait_ge(s_tr, G + g + 1)
                if g >= 2:
                    act.wait_ge(s_ct, g - 1)
                nc.scalar.activation(comb_up[:, g % 2, :], bank[g % 2][0:2 * half, :], ACT.Copy,
                                     scale=const[f"low_comb{layer}"][:, :]).then_inc(s_cu, 1)

    s_g, s_silu, s_u, s_w, s_cm, s_a, s_y, s_yt, s_ytr, s_x, s_hid = (
        sem(n) for n in ("gate_mm", "silu", "up_mm", "weigh", "comb_mm", "act_w", "down", "y_t", "y_tr", "x", "hid"))
    s_store = sem("store")
    GATE, UP, CB, YB, TB = [bank[0], bank[1]], [bank[2], bank[3]], [bank[4], bank[5]], bank[6], bank[7]

    with nc.Block() as block:

        @block.tensor
        def _(pe):
            def up(g, k, parity, first):
                n = (parity * nc_ + k) % 2
                x1, x2 = cols(x_hi, g), cols(x_lo, g)
                a = slice(k * P, (k + 1) * P)
                if not (first and k < 2):
                    pe.wait_ge(s_silu, g * nc_ + k - 1)
                for (hi, lo), dst, done in ((w["w1"], GATE[n], s_g), (w["w3"], UP[n], s_u)):
                    if done is s_u and not (first and k < 2):
                        pe.wait_ge(s_hid, g * nc_ + k - 1)
                    nc.tensor.matmul(dst[:, :], hi[:, a], x1, start=True, stop=False)
                    nc.tensor.matmul(dst[:, :], lo[:, a], x1, start=False, stop=False)
                    nc.tensor.matmul(dst[:, :], hi[:, a], x2, start=False, stop=True).then_inc(done, 1)
                pe.wait_ge(const["s_power"], 1)
                if not (first and k < 2):
                    pe.wait_ge(s_a, g * nc_ + k - 1)
                nc.tensor.matmul(CB[n][:, :], const[f"pick{layer}"][:, k, :], cols(comb_t, g),
                                 start=True, stop=True).then_inc(s_cm, 1)

            def down(g, k, parity, first):
                pe.wait_ge(s_a, g * nc_ + k + 1)
                if k == 0 and not first:
                    pe.wait_ge(s_yt, g)
                last_ = nc.tensor.matmul(YB[:, :], w["w2"][:, k, :], weighted[:, (parity * nc_ + k) % 2, :],
                                         start=(k == 0), stop=(k == nc_ - 1))
                last_.then_inc(s_y, 1)

            def back(g, parity, first):
                pe.wait_ge(s_yt, g + 1)
                if not first:
                    pe.wait_ge(s_x, g)
                for t in range(nt):
                    last_ = nc.tensor.transpose(TB[:, t * P:(t + 1) * P], y_t[:, parity, t * P:(t + 1) * P], ident[:])
                last_.then_inc(s_ytr, 1)

            def body(g, parity, first, last):
                for k in range(nc_):
                    if not (k == 0 and not first):
                        up(g, k, parity, first)
                    if k == 2 and not first:
                        back(g - 1, 1 - parity, False)
                    if k >= 1:
                        down(g, k - 1, parity, first)
                if not last:
                    up(g + 1, 0, 1 - parity, False)
                down(g, nc_ - 1, parity, first)

            body(0, 0, True, False)
            with pe.Fori(0, G // 2 - 1) as pair:
                body(2 * pair + 1, 1, False, False)
                body(2 * pair + 2, 0, False, False)
            body(G - 1, 1, False, True)
            back(G - 1, 1, False)

        def steps(loop, body):
            body(0, 0, True)
            with loop(0, G // 2 - 1) as pair:
                body(2 * pair + 1, 1, False)
                body(2 * pair + 2, 0, False)
            body(G - 1, 1, False)

        @block.scalar
        def _(act):
            def body(g, parity, first):
                for k in range(nc_):
                    n, slot = g * nc_ + k, (parity * nc_ + k) % 2
                    act.wait_ge(s_g, n + 1)
                    if not (first and k < 2):
                        act.wait_ge(s_hid, n - 1)
                    nc.scalar.activation(gate_act[:, slot, :], GATE[slot][:, :], ACT.Silu).then_inc(s_silu, 1)
                act.wait_ge(s_y, g * nc_ + nc_)
                if not first:
                    act.wait_ge(s_ytr, g)
                nc.scalar.activation(y_t[:, parity, :], YB[:, :], ACT.Copy).then_inc(s_yt, 1)

            steps(act.Fori, body)

        @block.vector
        def _(dve):
            def add(g):
                dve.wait_ge(s_ytr, g + 1)
                nc.vector.tensor_tensor(tiles(x_all, g), TB[:, :], tiles(x_all, g), ALU.add).then_inc(s_x, 1)

            def body(g, parity, first):
                for k in range(nc_):
                    n, slot = g * nc_ + k, (parity * nc_ + k) % 2
                    dve.wait_ge(s_silu, n + 1)
                    dve.wait_ge(s_u, n + 1)
                    nc.vector.tensor_tensor(hidden[:, slot, :], UP[slot][:, :], gate_act[:, slot, :],
                                            ALU.mult).then_inc(s_hid, 1)
                    dve.wait_ge(s_hid, n + 1)
                    dve.wait_ge(s_cm, n + 1)
                    if not (first and k < 2):
                        dve.wait_ge(s_y, n - 1)
                    nc.vector.tensor_tensor(weighted[:, slot, :], CB[slot][:, :], hidden[:, slot, :],
                                            ALU.mult).then_inc(s_a, 1)
                    if k == 3 and not first:
                        add(g - 1)

            steps(dve.Fori, body)
            add(G - 1)

        if out is not None:
            @block.sync
            def _(sp):
                for g in range(G):
                    sp.wait_ge(s_x, g + 1)
                    sp.dma_start(out[:, g * GB:(g + 1) * GB, :],
                                 x_all[:, g * GB * D:(g + 1) * GB * D].rearrange("p (b d) -> p b d", d=D)).then_inc(s_store, 16)
                sp.wait_ge(s_store, 16 * G)


def program(nc, a, out):
    with ExitStack() as mem:
        def sb(name, shape, dt=F32):
            return mem.enter_context(nc.sbuf_tensor(name, shape, dt))

        bank = [mem.enter_context(nc.psum_tensor(f"bank{i}", [P, 512], F32)) for i in range(8)]
        x_all = sb("x_all", [P, B * D])
        ctx_all = sb("ctx_all", [P, B * D])
        const = {
            "ident": sb("ident", [P, P]), "power": sb("power", [P, 1]), "eps": sb("eps", [P, 1]),
            "low": sb("low", [P, 2]), "mask": sb("mask", [P, B]),
            "low_comb0": sb("low_comb0", [64, 1]), "low_comb1": sb("low_comb1", [32, 1]),
        }
        gate0 = sb("gate0_hi", [P, E0], F32R), sb("gate0_lo", [P, E0], F32R)
        s_in, s_mk = (mem.enter_context(nc.semaphore(n)) for n in ("inputs", "mask_tr"))
        const["s_power"] = mem.enter_context(nc.semaphore("power_set"))

        def rounded(name, shape, dram, scope):
            t = scope.enter_context(nc.sbuf_tensor(name, shape, F32R))
            raw_ = scope.enter_context(nc.sbuf_tensor(name + "_raw", shape, F32))
            s1, s2 = (scope.enter_context(nc.semaphore(f"{name}_{i}")) for i in range(2))
            with nc.Block() as block:

                @block.sync
                def _(sp):
                    sp.dma_start(raw_[:], dram).then_inc(s1, 16)

                @block.scalar
                def _(act):
                    act.wait_ge(s1, 16)
                    nc.scalar.activation(t[:], raw_[:], ACT.Copy)
            return t

        maskt = sb("mask_rows", [B, P])
        with nc.Block() as block:

            @block.sync
            def _(sp):
                for dst, src in ((const["ident"][:, :], a["c_ident"]), (maskt[:, :], a["mask_BxS2_fk1"]),
                                 (const["low"][:, :], a["c_low"]), (const["low_comb0"][:, :], a["c_low_comb0"]),
                                 (const["low_comb1"][:, :], a["c_low_comb1"]),
                                 (x_all[:, :].rearrange("p (b d) -> p b d", d=D), a["x"].rearrange("b s d -> s b d")),
                                 (ctx_all[:, :].rearrange("p (b d) -> p b d", d=D),
                                  a["ctx_1024"].rearrange("b s d -> s b d"))):
                    sp.dma_start(dst, src).then_inc(s_in, 16)

            @block.tensor
            def _(pe):
                pe.wait_ge(s_in, 16 * 7)
                nc.tensor.transpose(bank[0][:, 0:B], maskt[:, :], const["ident"][0:B, 0:B]).then_inc(s_mk, 1)

            @block.vector
            def _(dve):
                nc.vector.memset(const["eps"][:, :], EPS)
                nc.vector.memset(const["power"][:, :], -0.5).then_inc(const["s_power"], 1)
                dve.wait_ge(s_mk, 1)
                nc.vector.tensor_copy(const["mask"][:, :], bank[0][:, 0:B])

        with ExitStack() as scope:
            def sc(name, shape, dt=F32):
                return scope.enter_context(nc.sbuf_tensor(name, shape, dt))

            const["sel"] = rounded("sel0", [P, 4, P], a["c_sel0"], scope)
            const["expand"] = sc("expand", [P, 512])
            w = {"wq": (sc("wq0_hi", [P, 512], F32R), sc("wq0_lo", [P, 512], F32R)),
                 "wk": (sc("wk0_hi", [P, 512], F32R), sc("wk0_lo", [P, 512], F32R)),
                 "wv": (sc("wv0_hi", [P, D], F32R), sc("wv0_lo", [P, D], F32R)),
                 "wo": sc("wo0", [P, 1, D]), "bias": sc("bias0", [P, 8]), "low_bias": sc("low_bias0", [P, 8]),
                 "bv": sc("bv0", [P, D]), "bo": sc("bo0", [P, D]), "gate": gate0}
            raw = {n: sc(f"raw_{n}", [P, P]) for n in ("wq", "wk", "wv", "wo")}
            raw["gate"], raw["b"] = sc("raw_gate", [E0, P]), sc("raw_b", [P, 2])
            load_and_split_plain(nc, scope, ((a["c_expand"], const["expand"][:, :]),
                                             (a["L0_xattn_bv"].partition_broadcast(P), w["bv"][:, :]),
                                             (a["L0_xattn_bo"].partition_broadcast(P), w["bo"][:, :])))
            layer0_weights(nc, scope, bank, const,
                           {"wq": a["L0_xattn_Wq"], "wk": a["L0_xattn_Wk"], "wv": a["L0_xattn_Wv"],
                            "wo": a["L0_xattn_Wo"], "gate": a["L0_ffn_gate_w"],
                            "bq": a["L0_xattn_bq"].unsqueeze(1), "bk": a["L0_xattn_bk"].unsqueeze(1)}, w, raw)
            attention(nc, scope, 0, bank, x_all, ctx_all, const, w)

        with ExitStack() as scope:
            def sc(name, shape, dt=F32):
                return scope.enter_context(nc.sbuf_tensor(name, shape, dt))

            n0 = E0 * I0
            w = {"w1": (sc("w1_hi", [P, n0], F32R), sc("w1_lo", [P, n0], F32R)),
                 "w3": (sc("w3_hi", [P, n0], F32R), sc("w3_lo", [P, n0], F32R)),
                 "w2": sc("w2", [P, n0 // P, D]), "ebias": sc("ebias", [P, E0]), "gate": gate0}
            with ExitStack() as staging:
                const["pick0"] = scope.enter_context(nc.sbuf_tensor("pick0", [64, n0 // P, P], F32R))
                load_and_split(nc, staging,
                               [(a["L0_ffn_w1"].rearrange("e h i -> h e i"), w["w1"][0][:, :], w["w1"][1][:, :]),
                                (a["L0_ffn_w3"].rearrange("e h i -> h e i"), w["w3"][0][:, :], w["w3"][1][:, :])],
                               [(a["L0_ffn_w2"].rearrange("e i h -> (e i) h").rearrange("(c p) h -> p c h", p=P), w["w2"][:, :, :]),
                                (a["L0_ffn_e_bias"].partition_broadcast(P), w["ebias"][:, :])])
                round_constant(nc, staging, const["pick0"], "pick0", a["c_pick0"])
            ffn(nc, scope, 0, bank, x_all, const, w, None)

        with ExitStack() as scope:
            def sc(name, shape, dt=F32):
                return scope.enter_context(nc.sbuf_tensor(name, shape, dt))

            w = {n: (sc(f"{n}1_hi", [P, H * D1], F32R), sc(f"{n}1_lo", [P, H * D1], F32R)) for n in ("wq", "wk", "wv")}
            w["wo"] = sc("wo1", [P, H * D1 // P, D])
            const["sel"] = scope.enter_context(nc.sbuf_tensor("sel1", [P, 8, P], F32R))
            with ExitStack() as staging:
                load_and_split(nc, staging,
                               [(a[f"L1_xattn_{m}"], w[n][0][:, :], w[n][1][:, :])
                                for n, m in (("wq", "Wq"), ("wk", "Wk"), ("wv", "Wv"))],
                               [(a["L1_xattn_Wo"].rearrange("(c p) h -> p c h", p=P), w["wo"][:, :, :])])
                round_constant(nc, staging, const["sel"], "sel1", a["c_sel1"])
            attention(nc, scope, 1, bank, x_all, ctx_all, const, w)

        with ExitStack() as scope:
            def sc(name, shape, dt=F32):
                return scope.enter_context(nc.sbuf_tensor(name, shape, dt))

            n1 = E1 * I1 + HS
            nr = E1 * I1
            w = {n: (sc(f"{n}f_hi", [P, n1], F32R), sc(f"{n}f_lo", [P, n1], F32R)) for n in ("w1", "w3")}
            w["gate"] = sc("gate1_hi", [P, E1], F32R), sc("gate1_lo", [P, E1], F32R)
            w["w2"] = sc("w2f", [P, n1 // P, D])
            const["pick1"] = scope.enter_context(nc.sbuf_tensor("pick1", [32, n1 // P, P], F32R))
            with ExitStack() as staging:
                pairs = []
                for n in ("1", "3"):
                    hi, lo = w["w" + n]
                    pairs.append((a["L1_ffn_w" + n].rearrange("e h i -> h e i"), hi[:, 0:nr], lo[:, 0:nr]))
                    pairs.append((a["L1_ffn_ws" + n], hi[:, nr:n1], lo[:, nr:n1]))
                pairs.append((a["L1_ffn_gate_w"], w["gate"][0][:, :], w["gate"][1][:, :]))
                load_and_split(nc, staging, pairs,
                               [(a["L1_ffn_w2"].rearrange("e i h -> (e i) h").rearrange("(c p) h -> p c h", p=P),
                                 w["w2"][:, 0:nr // P, :]),
                                (a["L1_ffn_ws2"], w["w2"][:, nr // P, :])])
                round_constant(nc, staging, const["pick1"], "pick1", a["c_pick1"])
            ffn(nc, scope, 1, bank, x_all, const, w, out.rearrange("b s d -> s b d"))


def load_and_split_plain(nc, mem, plain):
    s = mem.enter_context(nc.semaphore(f"plain_in_{nc.next_id()}"))
    with nc.Block() as block:

        @block.sync
        def _(sp):
            for src, dst in plain:
                sp.dma_start(dst, src).then_inc(s, 16)
            sp.wait_ge(s, 16 * len(plain))


def round_constant(nc, mem, t, name, dram):
    raw = mem.enter_context(nc.sbuf_tensor(name + "_raw", list(t.shape), F32))
    s = mem.enter_context(nc.semaphore(name + "_in"))
    with nc.Block() as block:

        @block.sync
        def _(sp):
            sp.dma_start(raw[:], dram).then_inc(s, 16)

        @block.scalar
        def _(act):
            act.wait_ge(s, 16)
            nc.scalar.activation(t[:], raw[:], ACT.Copy)


def constants():
    f = np.float32
    ident = np.eye(P, dtype=f)
    expand = np.zeros((P, 512), f)
    for h in range(H):
        ch, part = divmod(h, 4)
        for term in range(4):
            for d in range(D0):
                expand[h * D0 + d, ch * P + part * 32 + term * D0 + d] = 1
    term = np.arange(P) % 32 // D0
    low = np.stack([term >= 2, term % 2 == 1], 1).astype(f)
    rows = np.arange(P)
    sel0 = np.zeros((P, 4, P), f)
    sel1 = np.zeros((P, 8, P), f)
    for m in range(4):
        sel0[rows % 32 == m, m, :] = 1
    for m in range(8):
        sel1[rows % 64 == m, m, :] = 1
    pick0 = np.zeros((64, E0 * I0 // P, P), f)
    for n in range(E0 * I0):
        for h in range(2):
            pick0[h * 32 + n // I0, n // P, n % P] = 1
    pick1 = np.zeros((32, (E1 * I1 + HS) // P, P), f)
    for n in range(E1 * I1 + HS):
        e = n // I1 if n < E1 * I1 else E1
        for h in range(2):
            pick1[h * 16 + e, n // P, n % P] = 1
    return {"c_ident": ident, "c_expand": expand, "c_low": low, "c_sel0": sel0, "c_sel1": sel1,
            "c_pick0": pick0, "c_pick1": pick1,
            "c_low_comb0": (np.arange(64) >= 32).astype(f)[:, None],
            "c_low_comb1": (np.arange(32) >= 16).astype(f)[:, None]}


def kernel(**inputs):
    import concourse.bacc as bacc
    from concourse.bass_utils import run_bass_kernel_spmd

    nc = bacc.Bacc("TRN2", target_bir_lowering=False, num_devices=1)
    arrays = {n: np.ascontiguousarray(v) for n, v in inputs.items()}
    arrays.update(constants())
    args = {n: nc.dram_tensor(n, v.shape, F32, kind="ExternalInput").ap() for n, v in arrays.items()}
    out = nc.dram_tensor("out", (B, S, D), F32, kind="ExternalOutput").ap()
    program(nc, args, out)
    r = run_bass_kernel_spmd(nc, [arrays], core_ids=[0])
    return r.results[0]["out"]
```

```python
import concourse.bass as bass
from concourse import mybir
from contextlib import ExitStack

import math

import numpy as np

F32 = mybir.dt.float32
F32R = mybir.dt.float32r
F16 = mybir.dt.float16
ACT = mybir.ActivationFunctionType
ALU = mybir.AluOpType
AX = mybir.AxisListType

B, S, D = 32, 128, 128
P = 128
H = 16
D0, D1 = D // H, 64
GB = 4
G = B // GB
NU = 4
US = GB * NU
LEAD = 5
EPS = 1e-5
E0, I0, K0 = 32, 96, 4
E1, I1, K1, HS = 8, 64, 2, 128
TINY = 1e-37
LIFT = 64.0
LN_LIFT = math.log(LIFT)
NONE = -1e30


class Attn:

    def __init__(self, layer):
        self.layer = layer
        if layer == 0:
            self.rows, self.hd, self.nchunk = 32, D0, 4
        else:
            self.rows, self.hd, self.nchunk = 64, D1, 8
        self.scale = float(np.float32(1.0) / np.sqrt(np.float32(self.hd)))
        self.npart = P // self.rows
        self.natt = H * self.hd // 512 if layer else 1
        qk = [(kind, ch) for ch in range(self.nchunk) for kind in "qk"]
        v = [("v", n) for n in range(GB * H * self.hd // 512)] if layer else [("v", 0)]
        self.fills = [("x", 0), ("c", 0)] + qk + v
        per = len(qk) // 8
        self.slots = {1: [0, 1]}
        for n in range(len(qk)):
            self.slots.setdefault(2 + n // per, []).append(2 + n)
        for n in range(len(v)):
            self.slots.setdefault(10 + n // 2, []).append(2 + len(qk) + n)
        self.qk_done = 2 + len(qk)

    def unit(self, r):
        part = r if self.layer == 0 else r // 2
        first = 0 if self.layer == 0 else 4 * (r % 2)
        return [(first + i, part * self.rows, (first + i) * self.npart + part) for i in range(4)]


def attention(nc, mem, layer, bank, x_all, ctx_all, const, weights):
    c = Attn(layer)
    RW, HD = c.rows, c.hd
    NF = len(c.fills)
    T4 = GB * P

    def sb(name, shape, dt=F32):
        return mem.enter_context(nc.sbuf_tensor(f"{name}_l{layer}", shape, dt))

    def sem(name):
        return mem.enter_context(nc.semaphore(f"{name}_l{layer}"))

    ident = const["ident"]
    xhat = sb("xhat", [P, GB, D])
    ctxm = sb("ctxm", [P, GB, D])
    stats = sb("stats", [P, GB, 6])
    meanvar = sb("meanvar", [P, GB, 2])
    vareps = sb("vareps", [P, GB])
    invdev = sb("invdev", [P, GB])
    rstd = sb("rstd", [P, GB])
    x_hi, x_lo = sb("x_hi", [P, T4], F32R), sb("x_lo", [P, T4], F32R)
    c_hi, c_lo = sb("c_hi", [P, T4], F32R), sb("c_lo", [P, T4], F32R)
    q_a = sb("q_a", [P, 2, c.nchunk, T4], F16)
    k_a = sb("k_a", [P, 2, c.nchunk, T4], F16)
    if layer:
        q_b = sb("q_b", [P, 2, c.nchunk, T4], F16)
        k_b = sb("k_b", [P, 2, c.nchunk, T4], F16)
        mask_g = sb("mask_g", [P, 2, GB])
    else:
        rounded_qk = sb("rounded_qk", [P, 2, T4], F16)
    v_hi = sb("v_hi", [P, 2, GB, H, HD + 1], F16)
    v_lo = sb("v_lo", [P, 2, GB, H, HD + 1], F16)
    negmax = sb("negmax", [P, 2, P])
    negmax_t = sb("negmax_t", [P, 2, P], F16)
    probs = sb("probs", [P, 2, 512])
    p_hi, p_lo = sb("p_hi", [P, 2, 512], F16), sb("p_lo", [P, 2, 512], F16)
    rden = sb("rden", [P, 2, 4])
    den = sb("den", [P, 2, 4])
    att = sb("att", [P, 2, H * HD])
    att_t = sb("att_t", [P, H * HD])
    lift = sb("lift", [P, 1])

    M_BANK, T_BANK, PV_BANK, TR_BANK, PJ_BANK = [0, 1], [2, 3], 4, 5, [6, 7]

    s_stats, s_mv, s_var, s_rstd, s_xhat, s_ctx = (sem(n) for n in ("stats", "mv", "var", "rstd", "xhat", "ctx"))
    s_fill, s_upper, s_lower = sem("fill"), sem("upper"), sem("lower")
    s_max_mm, s_max = sem("max_mm"), sem("max")
    s_nmt_mm, s_nmt = sem("nmt_mm"), sem("nmt")
    s_scores, s_exp, s_exp_hi, s_exp_lo = sem("scores"), sem("exp"), sem("exp_hi"), sem("exp_lo")
    s_pv, s_den, s_rden, s_att = sem("pv"), sem("den"), sem("rden"), sem("att")
    s_att_mm, s_att_t, s_out_mm, s_x = sem("att_mm"), sem("att_t"), sem("out_mm"), sem("x")
    s_set, s_vcol = sem("set"), sem("vcol")
    s_apart = sem("apart")

    def steps(loop, prologue, body, tail):
        prologue()
        body(0, 0, first=True, last=False)
        with loop(0, G // 2 - 1) as pair:
            body(2 * pair + 1, 1, first=False, last=False)
            body(2 * pair + 2, 0, first=False, last=False)
        body(G - 1, 1, first=False, last=True)
        tail()

    def fill_bank(parity, i):
        return bank[PJ_BANK[(parity * NF + i) % 2]]

    def step_tiles(t, g):
        return t[:, bass.ds(g * (GB * D), GB * D)]

    with nc.Block() as block:

        @block.tensor
        def _(pe):
            def fill(g, parity, i):
                kind, n = c.fills[i]
                o = fill_bank(parity, i)
                if kind == "x":
                    pe.wait_ge(s_xhat, g + 1)
                if kind == "c":
                    pe.wait_ge(s_ctx, g + 1)
                if i == 2:
                    pe.wait_ge(s_lower, g * NF + 2)
                elif not (isinstance(g, int) and g == 0 and i < 2):
                    pe.wait_ge(s_lower, g * NF + i - 1)
                if kind in "xc":
                    src = xhat if kind == "x" else ctxm
                    for j in range(GB):
                        last_ = nc.tensor.transpose(o[:, j * P:(j + 1) * P], src[:, j, :], ident[:])
                elif kind in "qk":
                    w_hi, w_lo = weights["w" + kind]
                    m_hi, m_lo = (x_hi, x_lo) if kind == "q" else (c_hi, c_lo)
                    cols = slice(n * P, (n + 1) * P)
                    nc.tensor.matmul(o[:, :], w_hi[:, cols], m_hi[:, :], start=True, stop=False)
                    nc.tensor.matmul(o[:, :], w_hi[:, cols], m_lo[:, :], start=False, stop=False)
                    last_ = nc.tensor.matmul(o[:, :], w_lo[:, cols], m_hi[:, :], start=False, stop=True)
                elif layer:
                    w_hi, w_lo = weights["wv"]
                    j, half = divmod(n, 2)
                    cols, tok = slice(half * 512, (half + 1) * 512), slice(j * P, (j + 1) * P)
                    nc.tensor.matmul(o[:, :], c_hi[:, tok], w_hi[:, cols], start=True, stop=False)
                    nc.tensor.matmul(o[:, :], c_hi[:, tok], w_lo[:, cols], start=False, stop=False)
                    last_ = nc.tensor.matmul(o[:, :], c_lo[:, tok], w_hi[:, cols], start=False, stop=True)
                else:
                    w_hi, w_lo = weights["wv"]
                    for j in range(GB):
                        oj, tok = o[:, j * D:(j + 1) * D], slice(j * P, (j + 1) * P)
                        nc.tensor.matmul(oj, c_hi[:, tok], w_hi[:, :], start=True, stop=False)
                        nc.tensor.matmul(oj, c_hi[:, tok], w_lo[:, :], start=False, stop=False)
                        nc.tensor.matmul(oj, c_lo[:, tok], w_hi[:, :], start=False, stop=False)
                        last_ = nc.tensor.matmul(oj, const["ones"][:, :], weights["bv"][:, :], start=False, stop=True)
                last_.then_inc(s_fill, 1)

            def maxima(u, g, parity, t, wait):
                j, r = divmod(t, NU)
                if t == 0:
                    pe.wait_ge(s_lower, g * NF + c.qk_done)
                if wait:
                    pe.wait_ge(s_max, u - 1)
                tok = slice(j * P, (j + 1) * P)
                for i, (ch, row, _) in enumerate(c.unit(r)):
                    rows = slice(row, row + RW)
                    last_ = nc.tensor.matmul(bank[M_BANK[t % 2]][:, i * P:(i + 1) * P],
                                             q_a[rows, parity, ch, tok], k_a[rows, parity, ch, tok],
                                             start=True, stop=True)
                last_.then_inc(s_max_mm, 1)

            def transpose_maxima(b, j, wait):
                pe.wait_ge(s_max, NU * b + NU)
                if wait:
                    pe.wait_ge(s_x, b - 1)
                nc.tensor.transpose(bank[TR_BANK][:, 0:P], negmax[:, j % 2, :], ident[:]).then_inc(s_nmt_mm, 1)

            def scores(u, b, parity, s, wait):
                j, r = divmod(s, NU)
                if r == 0:
                    pe.wait_ge(s_nmt, b + 1)
                if wait:
                    pe.wait_ge(s_exp_hi, u - 1)
                tok = slice(j * P, (j + 1) * P)
                for i, (ch, row, _) in enumerate(c.unit(r)):
                    rows = slice(row, row + RW)
                    o = bank[T_BANK[r % 2]][:, i * P:(i + 1) * P]
                    ka, qa = k_a[rows, parity, ch, tok], q_a[rows, parity, ch, tok]
                    nc.tensor.matmul(o, ka, qa, start=True, stop=False)
                    if layer:
                        nc.tensor.matmul(o, ka, q_b[rows, parity, ch, tok], start=False, stop=False)
                        nc.tensor.matmul(o, k_b[rows, parity, ch, tok], qa, start=False, stop=False)
                    sel = const["sel"][rows, (i if layer == 0 else ch), :]
                    last_ = nc.tensor.matmul(o, sel, negmax_t[rows, j % 2, :], start=False, stop=True)
                last_.then_inc(s_scores, 1)

            def values(u, g, parity, s, wait):
                j, r = divmod(s, NU)
                if s == 0:
                    pe.wait_ge(s_lower, NF * g + NF)
                    if layer:
                        pe.wait_ge(s_vcol, g + 1)
                pe.wait_ge(s_exp_lo, u + 1)
                if wait:
                    pe.wait_ge(s_att, u)
                for i, (_, _, h) in enumerate(c.unit(r)):
                    o = bank[PV_BANK][:, i * (HD + 1):(i + 1) * (HD + 1)]
                    q = slice(i * P, (i + 1) * P)
                    nc.tensor.matmul(o, p_hi[:, r % 2, q], v_hi[:, parity, j, h, :], start=True, stop=False)
                    nc.tensor.matmul(o, p_hi[:, r % 2, q], v_lo[:, parity, j, h, :], start=False, stop=False)
                    last_ = nc.tensor.matmul(o, p_lo[:, r % 2, q], v_hi[:, parity, j, h, :], start=False, stop=True)
                last_.then_inc(s_pv, 1)

            def transpose_att(b, j, n):
                pe.wait_ge(s_att, NU * b + NU)
                if n:
                    pe.wait_ge(s_att_t, b * c.natt + n)
                for m in range(4 if layer else 1):
                    last_ = nc.tensor.transpose(bank[TR_BANK][:, m * P:(m + 1) * P],
                                                att[:, j % 2, (4 * n + m) * P:(4 * n + m + 1) * P], ident[:])
                last_.then_inc(s_att_mm, 1)

            def out(b):
                pe.wait_ge(s_att_t, b * c.natt + c.natt)
                n = H * HD // P
                o = bank[TR_BANK][:, 0:D]
                for m in range(n):
                    last_ = nc.tensor.matmul(o, att_t[:, m * P:(m + 1) * P], weights["wo"][:, m, :],
                                             start=(m == 0), stop=(layer == 1 and m == n - 1))
                if layer == 0:
                    last_ = nc.tensor.matmul(o, const["ones"][:, :], weights["bo"][:, :], start=False, stop=True)
                last_.then_inc(s_out_mm, 1)

            def prologue():
                for i in range(NF):
                    fill(0, 0, i)
                for t in range(LEAD):
                    maxima(t, 0, 0, t, wait=t >= 2)
                transpose_maxima(0, 0, wait=False)

            def body(g, parity, first, last):
                for s in range(US):
                    j, r = divmod(s, NU)
                    b, u = g * GB + j, g * US + s
                    prev = not (first and j == 0)
                    scores(u, b, parity, s, wait=not (first and s < 2))
                    if s:
                        values(u - 1, g, parity, s - 1, wait=not (first and s == 1))
                    elif not first:
                        values(u - 1, g - 1, 1 - parity, US - 1, wait=True)
                    if r == 1 and prev:
                        transpose_att(b - 1, (j - 1) % GB, 0)
                    if not last:
                        for i in c.slots.get(s, []):
                            fill(g + 1, 1 - parity, i)
                    if s + LEAD < US:
                        maxima(u + LEAD, g, parity, s + LEAD, wait=True)
                    elif not last:
                        maxima(u + LEAD, g + 1, 1 - parity, s + LEAD - US, wait=True)
                    if r == 1 and prev and c.natt == 2:
                        transpose_att(b - 1, (j - 1) % GB, 1)
                    if r == 2 and prev:
                        out(b - 1)
                    if r == NU - 1 and not (last and j == GB - 1):
                        transpose_maxima(b + 1, (j + 1) % GB, wait=prev)

            def tail():
                values(B * NU - 1, G - 1, 1, US - 1, wait=True)
                for n in range(c.natt):
                    transpose_att(B - 1, GB - 1, n)
                out(B - 1)

            steps(pe.Fori, prologue, body, tail)

        @block.scalar
        def _(act):
            def fill(g, parity, i):
                kind, n = c.fills[i]
                o = fill_bank(parity, i)
                act.wait_ge(s_fill, g * NF + i + 1)
                if kind in "xc":
                    nc.scalar.activation((x_hi if kind == "x" else c_hi)[:, :], o[:, :],
                                         ACT.Copy).then_inc(s_upper, 1)
                elif kind in "qk" and layer == 0:
                    m = "qk".index(kind)
                    nc.scalar.activation(rounded_qk[:, m, :], o[:, :], ACT.Identity,
                                         scale=const["low"][:, m:m + 1],
                                         bias=weights["low_bias"][:, 4 * m + n:4 * m + n + 1]).then_inc(s_upper, 1)
                elif kind in "qk":
                    nc.scalar.activation((q_a if kind == "q" else k_a)[:, parity, n, :], o[:, :],
                                         ACT.Copy).then_inc(s_upper, 1)
                elif layer:
                    j, half = divmod(n, 2)
                    nh = H // 2
                    nc.scalar.activation(v_hi[:, parity, j, half * nh:(half + 1) * nh, 0:HD],
                                         o[:, :].rearrange("p (h d) -> p h d", d=HD), ACT.Copy,
                                         scale=mask_g[:, parity, j:j + 1]).then_inc(s_upper, 1)
                else:
                    nc.scalar.activation(v_hi[:, parity, :, :, 0:HD].rearrange("p j h d -> p (j h) d"),
                                         o[:, :].rearrange("p (h d) -> p h d", d=HD), ACT.Copy).then_inc(s_upper, 1)

            def transposed_maxima(b, j):
                act.wait_ge(s_nmt_mm, b + 1)
                nc.scalar.activation(negmax_t[:, j % 2, :], bank[TR_BANK][:, 0:P], ACT.Copy).then_inc(s_nmt, 1)

            def exponentials(u, r, wait):
                act.wait_ge(s_scores, u + 1)
                if wait:
                    act.wait_ge(s_pv, u - 1)
                nc.scalar.activation(probs[:, r % 2, :], bank[T_BANK[r % 2]][:, :], ACT.Exp,
                                     scale=c.scale, bias=lift[:, :]).then_inc(s_exp, 1)
                nc.scalar.activation(p_hi[:, r % 2, :], bank[T_BANK[r % 2]][:, :], ACT.Exp,
                                     scale=c.scale, bias=lift[:, :]).then_inc(s_exp_hi, 1)

            def transposed_att(b, n):
                act.wait_ge(s_att_mm, b * c.natt + n + 1)
                width = 512 if layer else P
                nc.scalar.activation(att_t[:, n * 512:n * 512 + width], bank[TR_BANK][:, 0:width],
                                     ACT.Copy).then_inc(s_att_t, 1)

            def prologue():
                act.wait_ge(s_set, 1)
                if layer:
                    act.wait_ge(s_vcol, 1)
                for i in range(NF):
                    fill(0, 0, i)
                transposed_maxima(0, 0)

            def body(g, parity, first, last):
                for s in range(US):
                    j, r = divmod(s, NU)
                    b, u = g * GB + j, g * US + s
                    prev = not (first and j == 0)
                    exponentials(u, r, wait=not (first and s < 2))
                    if r == 1 and prev:
                        transposed_att(b - 1, 0)
                    if not last:
                        if layer and s == 10:
                            act.wait_ge(s_vcol, g + 2)
                            act.sem_inc(s_apart, 1)
                        for i in c.slots.get(s, []):
                            fill(g + 1, 1 - parity, i)
                    if r == 1 and prev and c.natt == 2:
                        transposed_att(b - 1, 1)
                    if r == NU - 1 and not (last and j == GB - 1):
                        transposed_maxima(b + 1, (j + 1) % GB)

            def tail():
                for n in range(c.natt):
                    transposed_att(B - 1, n)

            steps(act.Fori, prologue, body, tail)

        @block.vector
        def _(dve):
            def statistics(g):
                for j in range(GB):
                    last_ = nc.vector.bn_stats(stats[:, j, :], x_all[:, bass.ds((g * GB + j) * D, D)])
                last_.then_inc(s_stats, 1)
                dve.wait_ge(s_stats, g + 1)
                dve.sem_inc(s_apart, 1)
                for j in range(GB):
                    last_ = nc.vector.bn_aggr(meanvar[:, j, :], stats[:, j, :])
                last_.then_inc(s_mv, 1)

            def normalise(g):
                dve.wait_ge(s_rstd, g + 1)
                for j in range(GB):
                    last_ = nc.vector.tensor_scalar(xhat[:, j, :], x_all[:, bass.ds((g * GB + j) * D, D)],
                                                    meanvar[:, j, 0:1], rstd[:, j:j + 1],
                                                    ALU.subtract, ALU.mult)
                last_.then_inc(s_xhat, 1)

            def fill(g, parity, i):
                kind, n = c.fills[i]
                o = fill_bank(parity, i)
                dve.wait_ge(s_upper, g * NF + i + 1)
                if kind in "xc":
                    hi, lo = (x_hi, x_lo) if kind == "x" else (c_hi, c_lo)
                    last_ = nc.vector.tensor_tensor(lo[:, :], o[:, :], hi[:, :].bitcast(F32), ALU.subtract)
                elif kind in "qk" and layer == 0:
                    m = "qk".index(kind)
                    last_ = nc.vector.scalar_tensor_tensor(
                        (q_a if kind == "q" else k_a)[:, parity, n, :], o[:, :],
                        weights["bias"][:, 4 * m + n:4 * m + n + 1], rounded_qk[:, m, :], ALU.add, ALU.subtract)
                elif kind in "qk":
                    hi, lo = (q_a, q_b) if kind == "q" else (k_a, k_b)
                    last_ = nc.vector.tensor_tensor(lo[:, parity, n, :], o[:, :], hi[:, parity, n, :], ALU.subtract)
                elif layer:
                    j, half = divmod(n, 2)
                    heads = slice(half * (H // 2), (half + 1) * (H // 2))
                    last_ = nc.vector.scalar_tensor_tensor(
                        v_lo[:, parity, j, heads, 0:HD], o[:, :].rearrange("p (h d) -> p h d", d=HD),
                        mask_g[:, parity, j:j + 1], v_hi[:, parity, j, heads, 0:HD], ALU.mult, ALU.subtract)
                else:
                    last_ = nc.vector.tensor_tensor(
                        v_lo[:, parity, :, :, 0:HD].rearrange("p j h d -> p (j h) d"),
                        o[:, :].rearrange("p (h d) -> p h d", d=HD),
                        v_hi[:, parity, :, :, 0:HD].rearrange("p j h d -> p (j h) d"), ALU.subtract)
                last_.then_inc(s_lower, 1)

            def maxima(u, t):
                j, r = divmod(t, NU)
                dve.wait_ge(s_max_mm, u + 1)
                m0 = c.unit(r)[0][1] + (0 if layer == 0 else c.unit(r)[0][0])
                nc.vector.tensor_reduce(negmax[:, j % 2, m0:m0 + 4],
                                        bank[M_BANK[t % 2]][:, :].rearrange("p (a b) -> p a b", b=P),
                                        AX.X, ALU.max, negate=True).then_inc(s_max, 1)

            def attention_out(u, j, r):
                dve.wait_ge(s_pv, u + 1)
                o = bank[PV_BANK][:, 0:4 * (HD + 1)].rearrange("p (a b) -> p a b", b=HD + 1)
                nc.vector.tensor_scalar(den[:, r % 2, :], o[:, :, HD], TINY, None, ALU.max).then_inc(s_den, 1)
                dve.wait_ge(s_den, u + 1)
                nc.vector.reciprocal(rden[:, r % 2, :], den[:, r % 2, :]).then_inc(s_rden, 1)
                dve.wait_ge(s_rden, u + 1)
                h0 = c.unit(r)[0][2]
                dst = att[:, j % 2, :].rearrange("p (c n d) -> p c n d", n=c.npart, d=HD)
                dst = dst[:, h0 // c.npart:h0 // c.npart + 4, h0 % c.npart, :]
                nc.vector.tensor_tensor(dst, o[:, :, 0:HD],
                                        rden[:, r % 2, :].unsqueeze(2).broadcast_to([P, 4, HD]),
                                        ALU.mult).then_inc(s_att, 1)

            def add(b):
                dve.wait_ge(s_out_mm, b + 1)
                x_b = x_all[:, bass.ds(b * D, D)]
                nc.vector.tensor_tensor(x_b, bank[TR_BANK][:, 0:D], x_b, ALU.add).then_inc(s_x, 1)

            def prologue():
                nc.vector.memset(negmax[:, :, :], 0.0)
                nc.vector.memset(v_lo[:, :, :, :, HD], 0.0)
                if layer == 0:
                    nc.vector.memset(v_hi[:, :, :, :, HD], 1.0)
                nc.vector.memset(lift[:, :], LN_LIFT).then_inc(s_set, 1)
                dve.wait_ge(s_set, 1)
                statistics(0)
                normalise(0)
                for i in range(NF):
                    fill(0, 0, i)
                for t in range(LEAD):
                    maxima(t, t)

            def body(g, parity, first, last):
                for s in range(US):
                    j, r = divmod(s, NU)
                    b, u = g * GB + j, g * US + s
                    prev = not (first and j == 0)
                    if s == 0 and not last:
                        statistics(g + 1)
                    if s:
                        attention_out(u - 1, (s - 1) // NU, (s - 1) % NU)
                    elif not first:
                        attention_out(u - 1, GB - 1, NU - 1)
                    if not last:
                        for i in c.slots.get(s, []):
                            fill(g + 1, 1 - parity, i)
                    if not (last and s + LEAD >= US):
                        maxima(u + LEAD, (s + LEAD) % US)
                    if s == 0 and not last:
                        normalise(g + 1)
                    if r == 2 and prev:
                        add(b - 1)

            def tail():
                attention_out(B * NU - 1, GB - 1, NU - 1)
                add(B - 1)

            steps(dve.Fori, prologue, body, tail)

        @block.gpsimd
        def _(pool):
            def deviation(g):
                pool.wait_ge(s_mv, g + 1)
                nc.gpsimd.tensor_tensor(vareps[:, :], meanvar[:, :, 1], const["eps"][:, :].broadcast_to([P, GB]),
                                        ALU.add).then_inc(s_var, 1)
                pool.wait_ge(s_var, (2 if layer else 1) * g + 1)
                nc.gpsimd.tensor_tensor((invdev if layer else rstd)[:, :], vareps[:, :],
                                        const["power"][:, :].broadcast_to([P, GB]),
                                        ALU.pow).then_inc(s_var if layer else s_rstd, 1)
                if layer:
                    pool.wait_ge(s_var, 2 * g + 2)
                    pool.sem_inc(s_apart, 1)
                    nc.gpsimd.tensor_tensor(rstd[:, :], invdev[:, :], const["mask"][:, bass.ds(g * GB, GB)],
                                            ALU.mult).then_inc(s_rstd, 1)

            def context(g, parity, wait, values=False):
                if wait:
                    pool.wait_ge(s_fill, (g - 1) * NF + 2)
                    pool.sem_inc(s_apart, 1)
                if layer == 0:
                    nc.gpsimd.tensor_copy(ctxm[:, :, :].rearrange("p j d -> p (j d)"),
                                          step_tiles(ctx_all, g)).then_inc(s_ctx, 1)
                    return
                columns = const["mask"][:, bass.ds(g * GB, GB)]
                nc.gpsimd.tensor_tensor(ctxm[:, :, :], step_tiles(ctx_all, g).rearrange("p (j d) -> p j d", d=D),
                                        columns.unsqueeze(2).broadcast_to([P, GB, D]),
                                        ALU.mult).then_inc(s_ctx, 1)
                if values:
                    pool.wait_ge(s_pv, US * (g - 1))
                    pool.sem_inc(s_apart, 1)
                nc.gpsimd.tensor_copy(mask_g[:, parity, :], columns)
                nc.gpsimd.tensor_copy(v_hi[:, parity, :, :, HD],
                                      columns.unsqueeze(2).broadcast_to([P, GB, H])).then_inc(s_vcol, 1)

            def lower_probs(u, r):
                pool.wait_ge(s_exp_hi, u + 1)
                nc.gpsimd.tensor_tensor(p_lo[:, r % 2, :], probs[:, r % 2, :], p_hi[:, r % 2, :],
                                        ALU.subtract).then_inc(s_exp_lo, 1)

            def prologue():
                context(0, 0, wait=False)
                deviation(0)

            def body(g, parity, first, last):
                for s in range(US):
                    if s == 0 and not last:
                        deviation(g + 1)
                    lower_probs(g * US + s, s % NU)
                    if s == 0 and not last:
                        context(g + 1, 1 - parity, wait=True, values=not first)

            steps(pool.Fori, prologue, body, lambda: None)


def load_and_split(nc, mem, pairs, plain):
    widest = max(hi.shape[1] for _, hi, _ in pairs)
    stage = [mem.enter_context(nc.sbuf_tensor(f"stage_{nc.next_id()}", [P, widest], F32)) for _ in range(2)]
    s_in = [mem.enter_context(nc.semaphore(f"staged_{nc.next_id()}")) for _ in pairs]
    s_plain = mem.enter_context(nc.semaphore(f"plain_{nc.next_id()}"))
    s_hi = mem.enter_context(nc.semaphore(f"split_upper_{nc.next_id()}"))
    s_lo = mem.enter_context(nc.semaphore(f"split_lower_{nc.next_id()}"))
    with nc.Block() as block:

        @block.sync
        def _(sp):
            for n, (src, hi, _) in enumerate(pairs):
                if n >= 2:
                    sp.wait_ge(s_lo, n - 1)
                sp.dma_start(shaped(stage[n % 2][:, 0:hi.shape[1]], src), src).then_inc(s_in[n], 16)
            for src, dst in plain:
                sp.dma_start(dst, src).then_inc(s_plain, 16)
            sp.wait_ge(s_plain, 16 * len(plain))

        @block.scalar
        def _(act):
            for n, (_, hi, _) in enumerate(pairs):
                act.wait_ge(s_in[n], 16)
                nc.scalar.activation(hi, stage[n % 2][:, 0:hi.shape[1]], ACT.Copy).then_inc(s_hi, 1)

        @block.vector
        def _(dve):
            for n, (_, hi, lo) in enumerate(pairs):
                dve.wait_ge(s_hi, n + 1)
                nc.vector.tensor_tensor(lo, stage[n % 2][:, 0:hi.shape[1]], hi.bitcast(F32),
                                        ALU.subtract).then_inc(s_lo, 1)


def shaped(tile_view, src):
    if len(src.shape) == 2:
        return tile_view
    return tile_view.rearrange("p (a b) -> p a b", b=src.shape[2])


def layer0_weights(nc, mem, bank, const, d, w, raw):
    s_raw, s_mm, s_hi, s_lo, s_lb = (mem.enter_context(nc.semaphore(n)) for n in
                                     ("raw_in", "spread_mm", "spread_hi", "spread_lo", "low_bias_done"))
    with nc.Block() as block:

        @block.sync
        def _(sp):
            for n in ("wq", "wk", "wv", "wo", "gate"):
                sp.dma_start(raw[n][:, :], d[n]).then_inc(s_raw, 16)
            sp.dma_start(raw["b"][:, 0:1], d["bq"]).then_inc(s_raw, 16)
            sp.dma_start(raw["b"][:, 1:2], d["bk"]).then_inc(s_raw, 16)

        @block.tensor
        def _(pe):
            pe.wait_ge(s_raw, 16 * 7)
            nc.tensor.matmul(bank[0][:, :], raw["wq"][:, :], const["expand"][:, :],
                             start=True, stop=True).then_inc(s_mm, 1)
            nc.tensor.matmul(bank[1][:, :], raw["wk"][:, :], const["expand"][:, :],
                             start=True, stop=True).then_inc(s_mm, 1)
            nc.tensor.transpose(bank[2][:, 0:P], raw["wv"][:, :], const["ident"][:]).then_inc(s_mm, 1)
            nc.tensor.transpose(bank[3][:, 0:E0], raw["gate"][:, :], const["ident"][0:E0, 0:E0]).then_inc(s_mm, 1)
            nc.tensor.transpose(bank[4][:, 0:P], raw["wo"][:, :], const["ident"][:]).then_inc(s_mm, 1)
            for n in range(2):
                for ch in range(4):
                    last_ = nc.tensor.matmul(bank[5][:, 4 * n + ch:4 * n + ch + 1],
                                             const["expand"][:, ch * P:(ch + 1) * P], raw["b"][:, n:n + 1],
                                             start=True, stop=True)
            last_.then_inc(s_mm, 1)

        split = [(w["wq"], 512), (w["wk"], 512), (w["wv"], P), (w["gate"], E0)]

        @block.scalar
        def _(act):
            for n, ((hi, _), width) in enumerate(split):
                act.wait_ge(s_mm, n + 1)
                nc.scalar.activation(hi[:, :], bank[n][:, 0:width], ACT.Copy).then_inc(s_hi, 1)
            act.wait_ge(s_mm, 5)
            nc.scalar.activation(w["wo"][:, 0, :], bank[4][:, 0:P], ACT.Copy)

        @block.vector
        def _(dve):
            for n, ((hi, lo), width) in enumerate(split):
                dve.wait_ge(s_hi, n + 1)
                nc.vector.tensor_tensor(lo[:, :], bank[n][:, 0:width], hi[:, :].bitcast(F32),
                                        ALU.subtract).then_inc(s_lo, 1)
            dve.wait_ge(s_mm, 6)
            nc.vector.tensor_copy(w["bias"][:, :], bank[5][:, 0:8]).then_inc(s_lb, 1)
            dve.wait_ge(s_lb, 1)
            for n in range(2):
                nc.vector.tensor_scalar(w["low_bias"][:, 4 * n:4 * n + 4], w["bias"][:, 4 * n:4 * n + 4],
                                        const["low"][:, n:n + 1], None, ALU.mult)


def ffn(nc, mem, layer, bank, x_all, const, w, out):
    ne, width, topk = (E0, I0, K0) if layer == 0 else (E1, I1, K1)
    nc_ = ne * width // P + (0 if layer == 0 else HS // P)
    half = 32 if layer == 0 else 16
    nt = GB
    T = B * S

    def sb(name, shape, dt=F32):
        return mem.enter_context(nc.sbuf_tensor(f"{name}_f{layer}", shape, dt))

    def sem(name):
        return mem.enter_context(nc.semaphore(f"{name}_f{layer}"))

    ident = const["ident"]
    x_hi, x_lo = sb("x_hi", [P, T], F32R), sb("x_lo", [P, T], F32R)
    comb_t = sb("comb_t", [2 * half, T], F32R)
    comb_up = sb("comb_up", [2 * half, 2, 512], F32R)
    xhat = sb("xhat", [P, 2, nt, D])
    stats = sb("stats", [P, 2, nt, 6])
    meanvar = sb("meanvar", [P, 2, nt, 2])
    vareps = sb("vareps", [P, 2, nt])
    rstd = sb("rstd", [P, 2, nt])
    score = sb("score", [P, B, ne])
    biased = sb("biased", [P, B, ne + 4])
    top8 = sb("top8", [P, B, 8])
    top = sb("top", [P, B, 8])
    marked = sb("marked", [P, B, ne + 4])
    total = sb("total", [P, B])
    comb = sb("comb", [P, B, 2 * half])
    gate_act = sb("gate_act", [P, 2, 512])
    hidden = sb("hidden", [P, 2, 512])
    weighted = sb("weighted", [P, 2, 512])
    y_t = sb("y_t", [P, 2, 512])

    s_stats, s_mv, s_var, s_rstd, s_xhat = (sem(n) for n in ("stats", "mv", "var", "rstd", "xhat"))
    s_tr, s_up, s_low, s_route = sem("tr"), sem("up"), sem("low"), sem("route")

    def cols(t, g):
        return t[:, bass.ds(g * 512, 512)]

    def tiles(t, g):
        return t[:, bass.ds(g * nt * D, nt * D)]

    LB = bank[6], bank[7]

    with nc.Block() as block:

        @block.tensor
        def _(pe):
            def logits(g, i):
                pe.wait_ge(s_low, g + 1)
                for t in range(nt):
                    n = g * nt + t
                    o = LB[n * ne // 512][:, n * ne % 512:n * ne % 512 + ne]
                    a = slice(n * P, (n + 1) * P)
                    nc.tensor.matmul(o, x_hi[:, a], w["gate"][0][:, :], start=True, stop=False)
                    nc.tensor.matmul(o, x_hi[:, a], w["gate"][1][:, :], start=False, stop=False)
                    last_ = nc.tensor.matmul(o, x_lo[:, a], w["gate"][0][:, :], start=False, stop=True)
                last_.then_inc(s_route, 1)

            for g in range(G):
                pe.wait_ge(s_xhat, g + 1)
                if g >= 2:
                    pe.wait_ge(s_low, g - 1)
                for t in range(nt):
                    last_ = nc.tensor.transpose(bank[g % 2][:, t * P:(t + 1) * P], xhat[:, g % 2, t, :], ident[:])
                last_.then_inc(s_tr, 1)
                if g >= 1:
                    logits(g - 1, 0)
            logits(G - 1, 0)

        @block.scalar
        def _(act):
            for g in range(G):
                act.wait_ge(s_tr, g + 1)
                nc.scalar.activation(x_hi[:, g * 512:(g + 1) * 512], bank[g % 2][:, :], ACT.Copy).then_inc(s_up, 1)
            act.wait_ge(s_route, G)
            for n in range(0, B * ne, 512):
                m = min(512, B * ne)
                nc.scalar.activation(score[:, n // ne:(n + m) // ne, :],
                                     LB[n // 512][:, 0:m].rearrange("p (a b) -> p a b", b=ne), ACT.Sigmoid)

        @block.vector
        def _(dve):
            def norm(g):
                for t in range(nt):
                    last_ = nc.vector.bn_stats(stats[:, g % 2, t, :], x_all[:, (g * nt + t) * D:(g * nt + t + 1) * D])
                last_.then_inc(s_stats, 1)
                dve.wait_ge(s_stats, g + 1)
                for t in range(nt):
                    last_ = nc.vector.bn_aggr(meanvar[:, g % 2, t, :], stats[:, g % 2, t, :])
                last_.then_inc(s_mv, 1)

            norm(0)
            for g in range(G):
                if g + 1 < G:
                    norm(g + 1)
                dve.wait_ge(s_rstd, g + 1)
                if g >= 2:
                    dve.wait_ge(s_tr, g - 1)
                for t in range(nt):
                    last_ = nc.vector.tensor_scalar(xhat[:, g % 2, t, :],
                                                    x_all[:, (g * nt + t) * D:(g * nt + t + 1) * D],
                                                    meanvar[:, g % 2, t, 0:1], rstd[:, g % 2, t:t + 1],
                                                    ALU.subtract, ALU.mult)
                last_.then_inc(s_xhat, 1)
                dve.wait_ge(s_up, g + 1)
                nc.vector.tensor_tensor(x_lo[:, g * 512:(g + 1) * 512], bank[g % 2][:, :],
                                        x_hi[:, g * 512:(g + 1) * 512].bitcast(F32), ALU.subtract).then_inc(s_low, 1)

        @block.gpsimd
        def _(pool):
            for g in range(G):
                pool.wait_ge(s_mv, g + 1)
                nc.gpsimd.tensor_scalar(vareps[:, g % 2, :], meanvar[:, g % 2, :, 1], EPS, None,
                                        ALU.add).then_inc(s_var, 1)
                pool.wait_ge(s_var, g + 1)
                nc.gpsimd.tensor_tensor(rstd[:, g % 2, :], vareps[:, g % 2, :],
                                        const["power"][:, :].broadcast_to([P, nt]), ALU.pow).then_inc(s_rstd, 1)

    s_c, s_ct, s_cu = sem("choice"), sem("comb_tr"), sem("comb_up")
    s_comb = sem("comb")
    with nc.Block() as block:

        @block.vector
        def _(dve):
            done = [0]

            def after(instruction):
                done[0] += 1
                instruction.then_inc(s_c, 1)
                dve.wait_ge(s_c, done[0])

            nc.vector.memset(biased[:, :, ne:ne + 4], NONE)
            nc.vector.memset(top[:, :, topk:8], NONE)
            if layer == 0:
                after(nc.vector.tensor_tensor(biased[:, :, 0:ne], score[:, :, :],
                                              w["ebias"][:, :].unsqueeze(1).broadcast_to([P, B, ne]), ALU.add))
            else:
                after(nc.vector.tensor_copy(biased[:, :, 0:ne], score[:, :, :]))
                nc.vector.memset(top[:, :, topk:8], NONE)
            for t in range(B):
                last_ = nc.vector.max(top8[:, t, :], biased[:, t, 0:ne])
            after(last_)
            after(nc.vector.tensor_copy(top[:, :, 0:topk], top8[:, :, 0:topk]))
            for t in range(B):
                last_ = nc.vector.match_replace(marked[:, t, :], top[:, t, :], biased[:, t, :], 2.0 * NONE)
            after(last_)
            after(nc.vector.tensor_single_scalar(comb[:, :, 0:ne], marked[:, :, 0:ne], 1.5 * NONE, ALU.is_lt))
            after(nc.vector.tensor_tensor(score[:, :, :], comb[:, :, 0:ne], score[:, :, :], ALU.mult))
            after(nc.vector.tensor_reduce(total[:, :], score[:, :, :], AX.X, ALU.add))
            after(nc.vector.reciprocal(total[:, :], total[:, :]))
            for h in range(2):
                if layer:
                    nc.vector.memset(comb[:, :, h * half + ne:h * half + half], 1.0)
                last_ = nc.vector.tensor_tensor(comb[:, :, h * half:h * half + ne], score[:, :, :],
                                                total[:, :].unsqueeze(2).broadcast_to([P, B, ne]), ALU.mult)
            last_.then_inc(s_comb, 1)
            for g in range(G):
                dve.wait_ge(s_cu, g + 1)
                nc.vector.tensor_tensor(comb_t[:, g * 512:(g + 1) * 512], bank[g % 2][0:2 * half, :],
                                        comb_up[:, g % 2, :].bitcast(F32), ALU.subtract).then_inc(s_ct, 1)

        @block.tensor
        def _(pe):
            pe.wait_ge(s_comb, 1)
            for g in range(G):
                if g >= 2:
                    pe.wait_ge(s_ct, g - 1)
                for t in range(nt):
                    last_ = nc.tensor.transpose(bank[g % 2][0:2 * half, t * P:(t + 1) * P],
                                                comb[:, g * nt + t, :], ident[:])
                last_.then_inc(s_tr, 1)

        @block.scalar
        def _(act):
            for g in range(G):
                act.wait_ge(s_tr, G + g + 1)
                if g >= 2:
                    act.wait_ge(s_ct, g - 1)
                nc.scalar.activation(comb_up[:, g % 2, :], bank[g % 2][0:2 * half, :], ACT.Copy,
                                     scale=const[f"low_comb{layer}"][:, :]).then_inc(s_cu, 1)

    s_g, s_silu, s_u, s_w, s_cm, s_a, s_y, s_yt, s_ytr, s_x, s_hid = (
        sem(n) for n in ("gate_mm", "silu", "up_mm", "weigh", "comb_mm", "act_w", "down", "y_t", "y_tr", "x", "hid"))
    s_store = sem("store")
    GATE, UP, CB, YB, TB = [bank[0], bank[1]], [bank[2], bank[3]], [bank[4], bank[5]], bank[6], bank[7]

    with nc.Block() as block:

        @block.tensor
        def _(pe):
            def up(g, k, parity, first):
                n = (parity * nc_ + k) % 2
                x1, x2 = cols(x_hi, g), cols(x_lo, g)
                a = slice(k * P, (k + 1) * P)
                if not (first and k < 2):
                    pe.wait_ge(s_silu, g * nc_ + k - 1)
                for (hi, lo), dst, done in ((w["w1"], GATE[n], s_g), (w["w3"], UP[n], s_u)):
                    if done is s_u and not (first and k < 2):
                        pe.wait_ge(s_hid, g * nc_ + k - 1)
                    nc.tensor.matmul(dst[:, :], hi[:, a], x1, start=True, stop=False)
                    nc.tensor.matmul(dst[:, :], lo[:, a], x1, start=False, stop=False)
                    nc.tensor.matmul(dst[:, :], hi[:, a], x2, start=False, stop=True).then_inc(done, 1)
                pe.wait_ge(const["s_power"], 1)
                if not (first and k < 2):
                    pe.wait_ge(s_a, g * nc_ + k - 1)
                nc.tensor.matmul(CB[n][:, :], const[f"pick{layer}"][:, k, :], cols(comb_t, g),
                                 start=True, stop=True).then_inc(s_cm, 1)

            def down(g, k, parity, first):
                pe.wait_ge(s_a, g * nc_ + k + 1)
                if k == 0 and not first:
                    pe.wait_ge(s_yt, g)
                last_ = nc.tensor.matmul(YB[:, :], w["w2"][:, k, :], weighted[:, (parity * nc_ + k) % 2, :],
                                         start=(k == 0), stop=(k == nc_ - 1))
                last_.then_inc(s_y, 1)

            def back(g, parity, first):
                pe.wait_ge(s_yt, g + 1)
                if not first:
                    pe.wait_ge(s_x, g)
                for t in range(nt):
                    last_ = nc.tensor.transpose(TB[:, t * P:(t + 1) * P], y_t[:, parity, t * P:(t + 1) * P], ident[:])
                last_.then_inc(s_ytr, 1)

            def body(g, parity, first, last):
                for k in range(nc_):
                    if not (k == 0 and not first):
                        up(g, k, parity, first)
                    if k == 2 and not first:
                        back(g - 1, 1 - parity, False)
                    if k >= 1:
                        down(g, k - 1, parity, first)
                if not last:
                    up(g + 1, 0, 1 - parity, False)
                down(g, nc_ - 1, parity, first)

            body(0, 0, True, False)
            with pe.Fori(0, G // 2 - 1) as pair:
                body(2 * pair + 1, 1, False, False)
                body(2 * pair + 2, 0, False, False)
            body(G - 1, 1, False, True)
            back(G - 1, 1, False)

        def steps(loop, body):
            body(0, 0, True)
            with loop(0, G // 2 - 1) as pair:
                body(2 * pair + 1, 1, False)
                body(2 * pair + 2, 0, False)
            body(G - 1, 1, False)

        @block.scalar
        def _(act):
            def body(g, parity, first):
                for k in range(nc_):
                    n, slot = g * nc_ + k, (parity * nc_ + k) % 2
                    act.wait_ge(s_g, n + 1)
                    if not (first and k < 2):
                        act.wait_ge(s_hid, n - 1)
                    nc.scalar.activation(gate_act[:, slot, :], GATE[slot][:, :], ACT.Silu).then_inc(s_silu, 1)
                act.wait_ge(s_y, g * nc_ + nc_)
                if not first:
                    act.wait_ge(s_ytr, g)
                nc.scalar.activation(y_t[:, parity, :], YB[:, :], ACT.Copy).then_inc(s_yt, 1)

            steps(act.Fori, body)

        @block.vector
        def _(dve):
            def add(g):
                dve.wait_ge(s_ytr, g + 1)
                nc.vector.tensor_tensor(tiles(x_all, g), TB[:, :], tiles(x_all, g), ALU.add).then_inc(s_x, 1)

            def body(g, parity, first):
                for k in range(nc_):
                    n, slot = g * nc_ + k, (parity * nc_ + k) % 2
                    dve.wait_ge(s_silu, n + 1)
                    dve.wait_ge(s_u, n + 1)
                    nc.vector.tensor_tensor(hidden[:, slot, :], UP[slot][:, :], gate_act[:, slot, :],
                                            ALU.mult).then_inc(s_hid, 1)
                    dve.wait_ge(s_hid, n + 1)
                    dve.wait_ge(s_cm, n + 1)
                    if not (first and k < 2):
                        dve.wait_ge(s_y, n - 1)
                    nc.vector.tensor_tensor(weighted[:, slot, :], CB[slot][:, :], hidden[:, slot, :],
                                            ALU.mult).then_inc(s_a, 1)
                    if k == 3 and not first:
                        add(g - 1)

            steps(dve.Fori, body)
            add(G - 1)

        if out is not None:
            @block.sync
            def _(sp):
                for g in range(G):
                    sp.wait_ge(s_x, g + 1)
                    sp.dma_start(out[:, g * GB:(g + 1) * GB, :],
                                 x_all[:, g * GB * D:(g + 1) * GB * D].rearrange("p (b d) -> p b d", d=D)).then_inc(s_store, 16)
                sp.wait_ge(s_store, 16 * G)


def program(nc, a, out):
    with ExitStack() as mem:
        def sb(name, shape, dt=F32):
            return mem.enter_context(nc.sbuf_tensor(name, shape, dt))

        bank = [mem.enter_context(nc.psum_tensor(f"bank{i}", [P, 512], F32)) for i in range(8)]
        x_all = sb("x_all", [P, B * D])
        ctx_all = sb("ctx_all", [P, B * D])
        const = {
            "ident": sb("ident", [P, P]), "power": sb("power", [P, 1]), "ones": sb("ones", [1, P]), "eps": sb("eps", [P, 1]),
            "low": sb("low", [P, 2]), "mask": sb("mask", [P, B]),
            "low_comb0": sb("low_comb0", [64, 1]), "low_comb1": sb("low_comb1", [32, 1]),
        }
        gate0 = sb("gate0_hi", [P, E0], F32R), sb("gate0_lo", [P, E0], F32R)
        s_in, s_mk = (mem.enter_context(nc.semaphore(n)) for n in ("inputs", "mask_tr"))
        const["s_power"] = mem.enter_context(nc.semaphore("power_set"))

        def rounded(name, shape, dram, scope):
            t = scope.enter_context(nc.sbuf_tensor(name, shape, F16))
            raw_ = scope.enter_context(nc.sbuf_tensor(name + "_raw", shape, F32))
            s1, s2 = (scope.enter_context(nc.semaphore(f"{name}_{i}")) for i in range(2))
            with nc.Block() as block:

                @block.sync
                def _(sp):
                    sp.dma_start(raw_[:], dram).then_inc(s1, 16)

                @block.scalar
                def _(act):
                    act.wait_ge(s1, 16)
                    nc.scalar.activation(t[:], raw_[:], ACT.Copy)
            return t

        maskt = sb("mask_rows", [B, P])
        with nc.Block() as block:

            @block.sync
            def _(sp):
                for dst, src in ((const["ident"][:, :], a["c_ident"]), (maskt[:, :], a["mask_BxS2_fk1"]),
                                 (const["low"][:, :], a["c_low"]), (const["low_comb0"][:, :], a["c_low_comb0"]),
                                 (const["low_comb1"][:, :], a["c_low_comb1"]),
                                 (x_all[:, :].rearrange("p (b d) -> p b d", d=D), a["x"].rearrange("b s d -> s b d")),
                                 (ctx_all[:, :].rearrange("p (b d) -> p b d", d=D),
                                  a["ctx_1024"].rearrange("b s d -> s b d"))):
                    sp.dma_start(dst, src).then_inc(s_in, 16)

            @block.tensor
            def _(pe):
                pe.wait_ge(s_in, 16 * 7)
                nc.tensor.transpose(bank[0][:, 0:B], maskt[:, :], const["ident"][0:B, 0:B]).then_inc(s_mk, 1)

            @block.vector
            def _(dve):
                nc.vector.memset(const["eps"][:, :], EPS)
                nc.vector.memset(const["ones"][:, :], 1.0)
                nc.vector.memset(const["power"][:, :], -0.5).then_inc(const["s_power"], 1)
                dve.wait_ge(s_mk, 1)
                nc.vector.tensor_copy(const["mask"][:, :], bank[0][:, 0:B])

        with ExitStack() as scope:
            def sc(name, shape, dt=F32):
                return scope.enter_context(nc.sbuf_tensor(name, shape, dt))

            const["sel"] = rounded("sel0", [P, 4, P], a["c_sel0"], scope)
            const["expand"] = sc("expand", [P, 512])
            w = {"wq": (sc("wq0_hi", [P, 512], F32R), sc("wq0_lo", [P, 512], F32R)),
                 "wk": (sc("wk0_hi", [P, 512], F32R), sc("wk0_lo", [P, 512], F32R)),
                 "wv": (sc("wv0_hi", [P, D], F32R), sc("wv0_lo", [P, D], F32R)),
                 "wo": sc("wo0", [P, 1, D]), "bias": sc("bias0", [P, 8]), "low_bias": sc("low_bias0", [P, 8]),
                 "bv": sc("bv0", [1, D]), "bo": sc("bo0", [1, D]), "gate": gate0}
            raw = {n: sc(f"raw_{n}", [P, P]) for n in ("wq", "wk", "wv", "wo")}
            raw["gate"], raw["b"] = sc("raw_gate", [E0, P]), sc("raw_b", [P, 2])
            load_and_split_plain(nc, scope, ((a["c_expand"], const["expand"][:, :]),
                                             (a["L0_xattn_bv"].unsqueeze(0), w["bv"][:, :]),
                                             (a["L0_xattn_bo"].unsqueeze(0), w["bo"][:, :])))
            layer0_weights(nc, scope, bank, const,
                           {"wq": a["L0_xattn_Wq"], "wk": a["L0_xattn_Wk"], "wv": a["L0_xattn_Wv"],
                            "wo": a["L0_xattn_Wo"], "gate": a["L0_ffn_gate_w"],
                            "bq": a["L0_xattn_bq"].unsqueeze(1), "bk": a["L0_xattn_bk"].unsqueeze(1)}, w, raw)
            attention(nc, scope, 0, bank, x_all, ctx_all, const, w)

        with ExitStack() as scope:
            def sc(name, shape, dt=F32):
                return scope.enter_context(nc.sbuf_tensor(name, shape, dt))

            n0 = E0 * I0
            w = {"w1": (sc("w1_hi", [P, n0], F32R), sc("w1_lo", [P, n0], F32R)),
                 "w3": (sc("w3_hi", [P, n0], F32R), sc("w3_lo", [P, n0], F32R)),
                 "w2": sc("w2", [P, n0 // P, D]), "ebias": sc("ebias", [P, E0]), "gate": gate0}
            with ExitStack() as staging:
                const["pick0"] = scope.enter_context(nc.sbuf_tensor("pick0", [64, n0 // P, P], F32R))
                load_and_split(nc, staging,
                               [(a["L0_ffn_w1"].rearrange("e h i -> h e i"), w["w1"][0][:, :], w["w1"][1][:, :]),
                                (a["L0_ffn_w3"].rearrange("e h i -> h e i"), w["w3"][0][:, :], w["w3"][1][:, :])],
                               [(a["L0_ffn_w2"].rearrange("e i h -> (e i) h").rearrange("(c p) h -> p c h", p=P), w["w2"][:, :, :]),
                                (a["L0_ffn_e_bias"].partition_broadcast(P), w["ebias"][:, :])])
                round_constant(nc, staging, const["pick0"], "pick0", a["c_pick0"])
            ffn(nc, scope, 0, bank, x_all, const, w, None)

        with ExitStack() as scope:
            def sc(name, shape, dt=F32):
                return scope.enter_context(nc.sbuf_tensor(name, shape, dt))

            w = {n: (sc(f"{n}1_hi", [P, H * D1], F32R), sc(f"{n}1_lo", [P, H * D1], F32R)) for n in ("wq", "wk", "wv")}
            w["wo"] = sc("wo1", [P, H * D1 // P, D])
            const["sel"] = scope.enter_context(nc.sbuf_tensor("sel1", [P, 8, P], F16))
            with ExitStack() as staging:
                load_and_split(nc, staging,
                               [(a[f"L1_xattn_{m}"], w[n][0][:, :], w[n][1][:, :])
                                for n, m in (("wq", "Wq"), ("wk", "Wk"), ("wv", "Wv"))],
                               [(a["L1_xattn_Wo"].rearrange("(c p) h -> p c h", p=P), w["wo"][:, :, :])])
                round_constant(nc, staging, const["sel"], "sel1", a["c_sel1"])
            attention(nc, scope, 1, bank, x_all, ctx_all, const, w)

        with ExitStack() as scope:
            def sc(name, shape, dt=F32):
                return scope.enter_context(nc.sbuf_tensor(name, shape, dt))

            n1 = E1 * I1 + HS
            nr = E1 * I1
            w = {n: (sc(f"{n}f_hi", [P, n1], F32R), sc(f"{n}f_lo", [P, n1], F32R)) for n in ("w1", "w3")}
            w["gate"] = sc("gate1_hi", [P, E1], F32R), sc("gate1_lo", [P, E1], F32R)
            w["w2"] = sc("w2f", [P, n1 // P, D])
            const["pick1"] = scope.enter_context(nc.sbuf_tensor("pick1", [32, n1 // P, P], F32R))
            with ExitStack() as staging:
                pairs = []
                for n in ("1", "3"):
                    hi, lo = w["w" + n]
                    pairs.append((a["L1_ffn_w" + n].rearrange("e h i -> h e i"), hi[:, 0:nr], lo[:, 0:nr]))
                    pairs.append((a["L1_ffn_ws" + n], hi[:, nr:n1], lo[:, nr:n1]))
                pairs.append((a["L1_ffn_gate_w"], w["gate"][0][:, :], w["gate"][1][:, :]))
                load_and_split(nc, staging, pairs,
                               [(a["L1_ffn_w2"].rearrange("e i h -> (e i) h").rearrange("(c p) h -> p c h", p=P),
                                 w["w2"][:, 0:nr // P, :]),
                                (a["L1_ffn_ws2"], w["w2"][:, nr // P, :])])
                round_constant(nc, staging, const["pick1"], "pick1", a["c_pick1"])
            ffn(nc, scope, 1, bank, x_all, const, w, out.rearrange("b s d -> s b d"))


def load_and_split_plain(nc, mem, plain):
    s = mem.enter_context(nc.semaphore(f"plain_in_{nc.next_id()}"))
    with nc.Block() as block:

        @block.sync
        def _(sp):
            for src, dst in plain:
                sp.dma_start(dst, src).then_inc(s, 16)
            sp.wait_ge(s, 16 * len(plain))


def round_constant(nc, mem, t, name, dram):
    raw = mem.enter_context(nc.sbuf_tensor(name + "_raw", list(t.shape), F32))
    s = mem.enter_context(nc.semaphore(name + "_in"))
    with nc.Block() as block:

        @block.sync
        def _(sp):
            sp.dma_start(raw[:], dram).then_inc(s, 16)

        @block.scalar
        def _(act):
            act.wait_ge(s, 16)
            nc.scalar.activation(t[:], raw[:], ACT.Copy)


def constants():
    f = np.float32
    ident = np.eye(P, dtype=f)
    expand = np.zeros((P, 512), f)
    for h in range(H):
        ch, part = divmod(h, 4)
        for term in range(4):
            for d in range(D0):
                expand[h * D0 + d, ch * P + part * 32 + term * D0 + d] = 1
    term = np.arange(P) % 32 // D0
    low = np.stack([term >= 2, term % 2 == 1], 1).astype(f)
    rows = np.arange(P)
    sel0 = np.zeros((P, 4, P), f)
    sel1 = np.zeros((P, 8, P), f)
    for m in range(4):
        sel0[rows % 32 == m, m, :] = 1
    for m in range(8):
        sel1[rows % 64 == m, m, :] = 1
    pick0 = np.zeros((64, E0 * I0 // P, P), f)
    for n in range(E0 * I0):
        for h in range(2):
            pick0[h * 32 + n // I0, n // P, n % P] = 1
    pick1 = np.zeros((32, (E1 * I1 + HS) // P, P), f)
    for n in range(E1 * I1 + HS):
        e = n // I1 if n < E1 * I1 else E1
        for h in range(2):
            pick1[h * 16 + e, n // P, n % P] = 1
    return {"c_ident": ident, "c_expand": expand, "c_low": low, "c_sel0": sel0, "c_sel1": sel1,
            "c_pick0": pick0, "c_pick1": pick1,
            "c_low_comb0": (np.arange(64) >= 32).astype(f)[:, None],
            "c_low_comb1": (np.arange(32) >= 16).astype(f)[:, None]}


def kernel(**inputs):
    import concourse.bacc as bacc
    from concourse.bass_utils import run_bass_kernel_spmd

    nc = bacc.Bacc("TRN2", target_bir_lowering=False, num_devices=1)
    arrays = {n: np.ascontiguousarray(v) for n, v in inputs.items()}
    arrays.update(constants())
    args = {n: nc.dram_tensor(n, v.shape, F32, kind="ExternalInput").ap() for n, v in arrays.items()}
    out = nc.dram_tensor("out", (B, S, D), F32, kind="ExternalOutput").ap()
    program(nc, args, out)
    r = run_bass_kernel_spmd(nc, [arrays], core_ids=[0])
    return r.results[0]["out"]
```

```python
import concourse.bass as bass
from concourse import mybir
from contextlib import ExitStack

import math

import numpy as np

F32 = mybir.dt.float32
F32R = mybir.dt.float32r
F16 = mybir.dt.float16
ACT = mybir.ActivationFunctionType
ALU = mybir.AluOpType
AX = mybir.AxisListType

B, S, D = 32, 128, 128
P = 128
H = 16
D0, D1 = D // H, 64
GB = 4
G = B // GB
NU = 4
US = GB * NU
LEAD = 5
WARM_UP = 16
LAG = 2
EPS = 1e-5
E0, I0, K0 = 32, 96, 4
E1, I1, K1, HS = 8, 64, 2, 128
TINY = 1e-37
LIFT = 64.0
LN_LIFT = math.log(LIFT)
NONE = -1e30


class Attn:

    def __init__(self, layer):
        self.layer = layer
        if layer == 0:
            self.rows, self.hd, self.nchunk = P, D0, 4
        else:
            self.rows, self.hd, self.nchunk = 64, D1, 8
        self.scale = float(np.float32(1.0) / np.sqrt(np.float32(self.hd)))
        self.npart = 4 if layer == 0 else 2
        self.natt = H * self.hd // 512 if layer else 1
        qk = [(kind, ch) for ch in range(self.nchunk) for kind in "qk"]
        v = [("v", n) for n in range(GB * H * self.hd // 512)] if layer else [("v", 0)]
        self.fills = [("x", 0), ("c", 0)] + qk + v
        per = len(qk) // 8
        self.slots = {1: [0, 1]}
        for n in range(len(qk)):
            self.slots.setdefault(2 + n // per, []).append(2 + n)
        for n in range(len(v)):
            self.slots.setdefault(10 + n // 2, []).append(2 + len(qk) + n)
        self.qk_done = 2 + len(qk)

    def unit(self, r):
        if self.layer == 0:
            return [(r, 0, 4 * r + i) for i in range(4)]
        part, first = r // 2, 4 * (r % 2)
        return [(first + i, part * self.rows, (first + i) * self.npart + part) for i in range(4)]


def attention(nc, mem, layer, bank, x_all, ctx_all, const, weights):
    c = Attn(layer)
    RW, HD = c.rows, c.hd
    NF = len(c.fills)
    T4 = GB * P

    def sb(name, shape, dt=F32):
        return mem.enter_context(nc.sbuf_tensor(f"{name}_l{layer}", shape, dt))

    def sem(name):
        return mem.enter_context(nc.semaphore(f"{name}_l{layer}"))

    ident = const["ident"]
    xhat = sb("xhat", [P, GB, D])
    ctxm = sb("ctxm", [P, GB, D])
    stats = sb("stats", [P, GB, 6])
    meanvar = sb("meanvar", [P, GB, 2])
    vareps = sb("vareps", [P, GB])
    invdev = sb("invdev", [P, GB])
    rstd = sb("rstd", [P, GB])
    x_hi, x_lo = sb("x_hi", [P, T4], F32R), sb("x_lo", [P, T4], F32R)
    c_hi, c_lo = sb("c_hi", [P, T4], F32R), sb("c_lo", [P, T4], F32R)
    if layer:
        q_a = sb("q_a", [P, 2, c.nchunk, T4], F16)
    else:
        q_pad = sb("q_pad", [P, 2, c.nchunk, 4, T4], F16)
        q_row = sb("q_row", [P, T4], F16)
    k_a = sb("k_a", [P, 2, c.nchunk, T4], F16)
    if layer:
        q_b = sb("q_b", [P, 2, c.nchunk, T4], F16)
        k_b = sb("k_b", [P, 2, c.nchunk, T4], F16)
        mask_g = sb("mask_g", [P, 2, GB])
    else:
        rounded_qk = sb("rounded_qk", [P, 2, T4], F16)
    v_hi = sb("v_hi", [P, 2, GB, H, HD + 1], F16)
    v_lo = sb("v_lo", [P, 2, GB, H, HD + 1], F16)
    negmax = sb("negmax", [P, 2, P])
    negmax_t = sb("negmax_t", [P, 2, P], F16)
    probs = sb("probs", [P, NU, 512])
    p_hi, p_lo = sb("p_hi", [P, NU, 512], F16), sb("p_lo", [P, NU, 512], F16)
    rden = sb("rden", [P, 2, 4])
    den = sb("den", [P, 2, 4])
    att = sb("att", [P, 2, H * HD])
    att_t = sb("att_t", [P, H * HD])
    lift = sb("lift", [P, 1])

    M_BANK, T_BANK, PV_BANK, TR_BANK, PJ_BANK = [0, 1], [2, 3], 4, 5, [6, 7]

    s_stats, s_mv, s_var, s_rstd, s_xhat, s_ctx = (sem(n) for n in ("stats", "mv", "var", "rstd", "xhat", "ctx"))
    s_fill, s_upper, s_lower = sem("fill"), sem("upper"), sem("lower")
    s_max_mm, s_max = sem("max_mm"), sem("max")
    s_nmt_mm, s_nmt = sem("nmt_mm"), sem("nmt")
    s_scores, s_exp, s_exp_hi, s_exp_lo = sem("scores"), sem("exp"), sem("exp_hi"), sem("exp_lo")
    s_pv, s_den, s_rden, s_att = sem("pv"), sem("den"), sem("rden"), sem("att")
    s_att_mm, s_att_t, s_out_mm, s_x = sem("att_mm"), sem("att_t"), sem("out_mm"), sem("x")
    s_set, s_vcol, s_qrow = sem("set"), sem("vcol"), sem("qrow")
    s_apart = sem("apart")

    def steps(loop, prologue, body, tail):
        prologue()
        body(0, 0, first=True, last=False)
        with loop(0, G // 2 - 1) as pair:
            body(2 * pair + 1, 1, first=False, last=False)
            body(2 * pair + 2, 0, first=False, last=False)
        body(G - 1, 1, first=False, last=True)
        tail()

    def fill_bank(parity, i):
        return bank[PJ_BANK[(parity * NF + i) % 2]]

    def step_tiles(t, g):
        return t[:, bass.ds(g * (GB * D), GB * D)]

    with nc.Block() as block:

        @block.tensor
        def _(pe):
            def fill(g, parity, i):
                kind, n = c.fills[i]
                o = fill_bank(parity, i)
                if kind == "x":
                    pe.wait_ge(s_xhat, g + 1)
                if kind == "c":
                    pe.wait_ge(s_ctx, g + 1)
                if i == 2:
                    pe.wait_ge(s_lower, g * NF + 2)
                elif not (isinstance(g, int) and g == 0 and i < 2):
                    pe.wait_ge(s_lower, g * NF + i - 1)
                if kind in "xc":
                    src = xhat if kind == "x" else ctxm
                    for j in range(GB):
                        last_ = nc.tensor.transpose(o[:, j * P:(j + 1) * P], src[:, j, :], ident[:])
                elif kind in "qk":
                    w_hi, w_lo = weights["w" + kind]
                    m_hi, m_lo = (x_hi, x_lo) if kind == "q" else (c_hi, c_lo)
                    cols = slice(n * P, (n + 1) * P)
                    nc.tensor.matmul(o[:, :], w_hi[:, cols], m_hi[:, :], start=True, stop=False)
                    nc.tensor.matmul(o[:, :], w_hi[:, cols], m_lo[:, :], start=False, stop=False)
                    last_ = nc.tensor.matmul(o[:, :], w_lo[:, cols], m_hi[:, :], start=False, stop=True)
                elif layer:
                    w_hi, w_lo = weights["wv"]
                    j, half = divmod(n, 2)
                    cols, tok = slice(half * 512, (half + 1) * 512), slice(j * P, (j + 1) * P)
                    nc.tensor.matmul(o[:, :], c_hi[:, tok], w_hi[:, cols], start=True, stop=False)
                    nc.tensor.matmul(o[:, :], c_hi[:, tok], w_lo[:, cols], start=False, stop=False)
                    last_ = nc.tensor.matmul(o[:, :], c_lo[:, tok], w_hi[:, cols], start=False, stop=True)
                else:
                    w_hi, w_lo = weights["wv"]
                    for j in range(GB):
                        oj, tok = o[:, j * D:(j + 1) * D], slice(j * P, (j + 1) * P)
                        nc.tensor.matmul(oj, c_hi[:, tok], w_hi[:, :], start=True, stop=False)
                        nc.tensor.matmul(oj, c_hi[:, tok], w_lo[:, :], start=False, stop=False)
                        nc.tensor.matmul(oj, c_lo[:, tok], w_hi[:, :], start=False, stop=False)
                        last_ = nc.tensor.matmul(oj, const["ones"][:, :], weights["bv"][:, :], start=False, stop=True)
                last_.then_inc(s_fill, 1)

            def maxima(u, g, parity, t, wait):
                j, r = divmod(t, NU)
                if t == 0:
                    pe.wait_ge(s_lower, g * NF + c.qk_done)
                if wait:
                    pe.wait_ge(s_max, u - 1)
                tok = slice(j * P, (j + 1) * P)
                for i, (ch, row, _) in enumerate(c.unit(r)):
                    rows = slice(row, row + RW)
                    qa = q_a[rows, parity, ch, tok] if layer else q_pad[:, parity, ch, i, tok]
                    last_ = nc.tensor.matmul(bank[M_BANK[t % 2]][:, i * P:(i + 1) * P],
                                             qa, k_a[rows, parity, ch, tok], start=True, stop=True)
                last_.then_inc(s_max_mm, 1)

            def transpose_maxima(b, j, wait):
                pe.wait_ge(s_max, NU * b + NU)
                if wait:
                    pe.wait_ge(s_x, b - 1)
                nc.tensor.transpose(bank[TR_BANK][:, 0:P], negmax[:, j % 2, :], ident[:]).then_inc(s_nmt_mm, 1)

            def scores(u, b, parity, s, wait):
                j, r = divmod(s, NU)
                if r == 0:
                    pe.wait_ge(s_nmt, b + 1)
                if wait:
                    pe.wait_ge(s_exp_hi, u - 1)
                tok = slice(j * P, (j + 1) * P)
                if layer == 0:
                    nc.tensor.matmul(bank[T_BANK[r % 2]][:, :], k_a[:, parity, r, tok], q_pad[:, parity, r, :, tok],
                                     start=True, stop=False)
                for i, (ch, row, _) in enumerate(c.unit(r)):
                    rows = slice(row, row + RW)
                    o = bank[T_BANK[r % 2]][:, i * P:(i + 1) * P]
                    if layer:
                        ka, qa = k_a[rows, parity, ch, tok], q_a[rows, parity, ch, tok]
                        nc.tensor.matmul(o, ka, qa, start=True, stop=False)
                        nc.tensor.matmul(o, ka, q_b[rows, parity, ch, tok], start=False, stop=False)
                        nc.tensor.matmul(o, k_b[rows, parity, ch, tok], qa, start=False, stop=False)
                    sel = const["sel"][rows, (4 * r + i if layer == 0 else ch), :]
                    last_ = nc.tensor.matmul(o, sel, negmax_t[rows, j % 2, :], start=False, stop=layer == 1 or i == 3)
                last_.then_inc(s_scores, 1)

            def values(u, g, parity, s, wait):
                j, r = divmod(s, NU)
                if s == 0:
                    pe.wait_ge(s_lower, NF * g + NF)
                    if layer:
                        pe.wait_ge(s_vcol, g + 1)
                pe.wait_ge(s_exp_lo, u + 1)
                if wait:
                    pe.wait_ge(s_att, u)
                for i, (_, _, h) in enumerate(c.unit(r)):
                    o = bank[PV_BANK][:, i * (HD + 1):(i + 1) * (HD + 1)]
                    q = slice(i * P, (i + 1) * P)
                    nc.tensor.matmul(o, p_hi[:, r, q], v_hi[:, parity, j, h, :], start=True, stop=False)
                    nc.tensor.matmul(o, p_hi[:, r, q], v_lo[:, parity, j, h, :], start=False, stop=False)
                    last_ = nc.tensor.matmul(o, p_lo[:, r, q], v_hi[:, parity, j, h, :], start=False, stop=True)
                last_.then_inc(s_pv, 1)

            def transpose_att(b, j, n):
                pe.wait_ge(s_att, NU * b + NU)
                if n:
                    pe.wait_ge(s_att_t, b * c.natt + n)
                for m in range(4 if layer else 1):
                    last_ = nc.tensor.transpose(bank[TR_BANK][:, m * P:(m + 1) * P],
                                                att[:, j % 2, (4 * n + m) * P:(4 * n + m + 1) * P], ident[:])
                last_.then_inc(s_att_mm, 1)

            def out(b):
                pe.wait_ge(s_att_t, b * c.natt + c.natt)
                n = H * HD // P
                o = bank[TR_BANK][:, 0:D]
                for m in range(n):
                    last_ = nc.tensor.matmul(o, att_t[:, m * P:(m + 1) * P], weights["wo"][:, m, :],
                                             start=(m == 0), stop=(layer == 1 and m == n - 1))
                if layer == 0:
                    last_ = nc.tensor.matmul(o, const["ones"][:, :], weights["bo"][:, :], start=False, stop=True)
                last_.then_inc(s_out_mm, 1)

            def prologue():
                for i in range(NF):
                    fill(0, 0, i)
                for t in range(LEAD):
                    maxima(t, 0, 0, t, wait=t >= 2)
                transpose_maxima(0, 0, wait=False)
                if layer == 0:
                    for _ in range(WARM_UP):
                        nc.tensor.matmul(bank[PV_BANK][:, :], k_a[:, 0, 0, 0:P], k_a[:, 0, 0, :], start=True, stop=True)

            def body(g, parity, first, last):
                for s in range(US):
                    j, r = divmod(s, NU)
                    b, u = g * GB + j, g * US + s
                    prev = not (first and j == 0)
                    scores(u, b, parity, s, wait=not (first and s < 2))
                    if s >= LAG:
                        values(u - LAG, g, parity, s - LAG, wait=not (first and s == LAG))
                    elif not first:
                        values(u - LAG, g - 1, 1 - parity, US + s - LAG, wait=True)
                    if r == 2 and prev:
                        transpose_att(b - 1, (j - 1) % GB, 0)
                    if r == 3 and prev:
                        out(b - 1)
                    if not last:
                        for i in c.slots.get(s, []):
                            fill(g + 1, 1 - parity, i)
                    if s + LEAD < US:
                        maxima(u + LEAD, g, parity, s + LEAD, wait=True)
                    elif not last:
                        maxima(u + LEAD, g + 1, 1 - parity, s + LEAD - US, wait=True)
                    if r == 2 and prev and c.natt == 2:
                        transpose_att(b - 1, (j - 1) % GB, 1)
                    if r == NU - 1 and not (last and j == GB - 1):
                        transpose_maxima(b + 1, (j + 1) % GB, wait=prev)

            def tail():
                for n in range(LAG, 0, -1):
                    values(B * NU - n, G - 1, 1, US - n, wait=True)
                for n in range(c.natt):
                    transpose_att(B - 1, GB - 1, n)
                out(B - 1)

            steps(pe.Fori, prologue, body, tail)

        @block.scalar
        def _(act):
            def fill(g, parity, i):
                kind, n = c.fills[i]
                o = fill_bank(parity, i)
                act.wait_ge(s_fill, g * NF + i + 1)
                if kind in "xc":
                    nc.scalar.activation((x_hi if kind == "x" else c_hi)[:, :], o[:, :],
                                         ACT.Copy).then_inc(s_upper, 1)
                elif kind in "qk" and layer == 0:
                    m = "qk".index(kind)
                    nc.scalar.activation(rounded_qk[:, m, :], o[:, :], ACT.Identity,
                                         scale=const["low"][:, m:m + 1],
                                         bias=weights["low_bias"][:, 4 * m + n:4 * m + n + 1]).then_inc(s_upper, 1)
                elif kind in "qk":
                    nc.scalar.activation((q_a if kind == "q" else k_a)[:, parity, n, :], o[:, :],
                                         ACT.Copy).then_inc(s_upper, 1)
                elif layer:
                    j, half = divmod(n, 2)
                    nh = H // 2
                    nc.scalar.activation(v_hi[:, parity, j, half * nh:(half + 1) * nh, 0:HD],
                                         o[:, :].rearrange("p (h d) -> p h d", d=HD), ACT.Copy,
                                         scale=mask_g[:, parity, j:j + 1]).then_inc(s_upper, 1)
                else:
                    nc.scalar.activation(v_hi[:, parity, :, :, 0:HD].rearrange("p j h d -> p (j h) d"),
                                         o[:, :].rearrange("p (h d) -> p h d", d=HD), ACT.Copy).then_inc(s_upper, 1)

            def transposed_maxima(b, j):
                act.wait_ge(s_nmt_mm, b + 1)
                nc.scalar.activation(negmax_t[:, j % 2, :], bank[TR_BANK][:, 0:P], ACT.Copy).then_inc(s_nmt, 1)

            def exponentials(u, r, wait):
                act.wait_ge(s_scores, u + 1)
                if wait:
                    act.wait_ge(s_pv, u - NU + 1)
                nc.scalar.activation(probs[:, r, :], bank[T_BANK[r % 2]][:, :], ACT.Exp,
                                     scale=c.scale, bias=lift[:, :]).then_inc(s_exp, 1)
                nc.scalar.activation(p_hi[:, r, :], bank[T_BANK[r % 2]][:, :], ACT.Exp,
                                     scale=c.scale, bias=lift[:, :]).then_inc(s_exp_hi, 1)

            def transposed_att(b, n):
                act.wait_ge(s_att_mm, b * c.natt + n + 1)
                width = 512 if layer else P
                nc.scalar.activation(att_t[:, n * 512:n * 512 + width], bank[TR_BANK][:, 0:width],
                                     ACT.Copy).then_inc(s_att_t, 1)

            def prologue():
                act.wait_ge(s_set, 1)
                if layer:
                    act.wait_ge(s_vcol, 1)
                for i in range(NF):
                    fill(0, 0, i)
                transposed_maxima(0, 0)

            def body(g, parity, first, last):
                for s in range(US):
                    j, r = divmod(s, NU)
                    b, u = g * GB + j, g * US + s
                    prev = not (first and j == 0)
                    exponentials(u, r, wait=not (first and s < NU))
                    if r == 2 and prev:
                        transposed_att(b - 1, 0)
                    if not last:
                        if layer and s == 10:
                            act.wait_ge(s_vcol, g + 2)
                            act.sem_inc(s_apart, 1)
                        for i in c.slots.get(s, []):
                            fill(g + 1, 1 - parity, i)
                    if r == 2 and prev and c.natt == 2:
                        transposed_att(b - 1, 1)
                    if r == NU - 1 and not (last and j == GB - 1):
                        transposed_maxima(b + 1, (j + 1) % GB)

            def tail():
                for n in range(c.natt):
                    transposed_att(B - 1, n)

            steps(act.Fori, prologue, body, tail)

        @block.vector
        def _(dve):
            def statistics(g):
                for j in range(GB):
                    last_ = nc.vector.bn_stats(stats[:, j, :], x_all[:, bass.ds((g * GB + j) * D, D)])
                last_.then_inc(s_stats, 1)
                dve.wait_ge(s_stats, g + 1)
                dve.sem_inc(s_apart, 1)
                for j in range(GB):
                    last_ = nc.vector.bn_aggr(meanvar[:, j, :], stats[:, j, :])
                last_.then_inc(s_mv, 1)

            def normalise(g):
                dve.wait_ge(s_rstd, g + 1)
                for j in range(GB):
                    last_ = nc.vector.tensor_scalar(xhat[:, j, :], x_all[:, bass.ds((g * GB + j) * D, D)],
                                                    meanvar[:, j, 0:1], rstd[:, j:j + 1],
                                                    ALU.subtract, ALU.mult)
                last_.then_inc(s_xhat, 1)

            def fill(g, parity, i):
                kind, n = c.fills[i]
                o = fill_bank(parity, i)
                dve.wait_ge(s_upper, g * NF + i + 1)
                if kind in "xc":
                    hi, lo = (x_hi, x_lo) if kind == "x" else (c_hi, c_lo)
                    last_ = nc.vector.tensor_tensor(lo[:, :], o[:, :], hi[:, :].bitcast(F32), ALU.subtract)
                elif kind in "qk" and layer == 0:
                    m = "qk".index(kind)
                    last_ = nc.vector.scalar_tensor_tensor(
                        q_row[:, :] if kind == "q" else k_a[:, parity, n, :], o[:, :],
                        weights["bias"][:, 4 * m + n:4 * m + n + 1], rounded_qk[:, m, :], ALU.add, ALU.subtract)
                    if kind == "q":
                        last_.then_inc(s_qrow, 1)
                        dve.wait_ge(s_qrow, g * c.nchunk + n + 1)
                        for part in range(4):
                            last_ = nc.vector.tensor_scalar(q_pad[:, parity, n, part, :], q_row[:, :],
                                                            const["quarter"][:, part:part + 1], None, ALU.mult)
                elif kind in "qk":
                    hi, lo = (q_a, q_b) if kind == "q" else (k_a, k_b)
                    last_ = nc.vector.tensor_tensor(lo[:, parity, n, :], o[:, :], hi[:, parity, n, :], ALU.subtract)
                elif layer:
                    j, half = divmod(n, 2)
                    heads = slice(half * (H // 2), (half + 1) * (H // 2))
                    last_ = nc.vector.scalar_tensor_tensor(
                        v_lo[:, parity, j, heads, 0:HD], o[:, :].rearrange("p (h d) -> p h d", d=HD),
                        mask_g[:, parity, j:j + 1], v_hi[:, parity, j, heads, 0:HD], ALU.mult, ALU.subtract)
                else:
                    last_ = nc.vector.tensor_tensor(
                        v_lo[:, parity, :, :, 0:HD].rearrange("p j h d -> p (j h) d"),
                        o[:, :].rearrange("p (h d) -> p h d", d=HD),
                        v_hi[:, parity, :, :, 0:HD].rearrange("p j h d -> p (j h) d"), ALU.subtract)
                last_.then_inc(s_lower, 1)

            def maxima(u, t):
                j, r = divmod(t, NU)
                dve.wait_ge(s_max_mm, u + 1)
                m0 = 4 * r if layer == 0 else c.unit(r)[0][1] + c.unit(r)[0][0]
                nc.vector.tensor_reduce(negmax[:, j % 2, m0:m0 + 4],
                                        bank[M_BANK[t % 2]][:, :].rearrange("p (a b) -> p a b", b=P),
                                        AX.X, ALU.max, negate=True).then_inc(s_max, 1)

            def attention_out(u, j, r):
                dve.wait_ge(s_pv, u + 1)
                o = bank[PV_BANK][:, 0:4 * (HD + 1)].rearrange("p (a b) -> p a b", b=HD + 1)
                nc.vector.tensor_scalar(den[:, r % 2, :], o[:, :, HD], TINY, None, ALU.max).then_inc(s_den, 1)
                dve.wait_ge(s_den, u + 1)
                nc.vector.reciprocal(rden[:, r % 2, :], den[:, r % 2, :]).then_inc(s_rden, 1)
                dve.wait_ge(s_rden, u + 1)
                h0 = c.unit(r)[0][2]
                if layer == 0:
                    dst = att[:, j % 2, h0 * HD:(h0 + 4) * HD].rearrange("p (h d) -> p h d", d=HD)
                else:
                    dst = att[:, j % 2, :].rearrange("p (c n d) -> p c n d", n=c.npart, d=HD)
                    dst = dst[:, h0 // c.npart:h0 // c.npart + 4, h0 % c.npart, :]
                nc.vector.tensor_tensor(dst, o[:, :, 0:HD],
                                        rden[:, r % 2, :].unsqueeze(2).broadcast_to([P, 4, HD]),
                                        ALU.mult).then_inc(s_att, 1)

            def add(b):
                dve.wait_ge(s_out_mm, b + 1)
                x_b = x_all[:, bass.ds(b * D, D)]
                nc.vector.tensor_tensor(x_b, bank[TR_BANK][:, 0:D], x_b, ALU.add).then_inc(s_x, 1)

            def prologue():
                nc.vector.memset(negmax[:, :, :], 0.0)
                nc.vector.memset(v_lo[:, :, :, :, HD], 0.0)
                if layer == 0:
                    nc.vector.memset(v_hi[:, :, :, :, HD], 1.0)
                nc.vector.memset(lift[:, :], LN_LIFT).then_inc(s_set, 1)
                dve.wait_ge(s_set, 1)
                statistics(0)
                normalise(0)
                for i in range(NF):
                    fill(0, 0, i)
                for t in range(LEAD):
                    maxima(t, t)

            def body(g, parity, first, last):
                for s in range(US):
                    j, r = divmod(s, NU)
                    b, u = g * GB + j, g * US + s
                    prev = not (first and j == 0)
                    if s == 0 and not last:
                        statistics(g + 1)
                    if not (first and s < LAG):
                        t = (s - LAG) % US
                        attention_out(u - LAG, t // NU, t % NU)
                    if r == 3 and prev:
                        add(b - 1)
                    if not last:
                        for i in c.slots.get(s, []):
                            fill(g + 1, 1 - parity, i)
                    if not (last and s + LEAD >= US):
                        maxima(u + LEAD, (s + LEAD) % US)
                    if s == 0 and not last:
                        normalise(g + 1)

            def tail():
                for n in range(LAG, 0, -1):
                    attention_out(B * NU - n, GB - 1, NU - n)
                add(B - 1)

            steps(dve.Fori, prologue, body, tail)

        @block.gpsimd
        def _(pool):
            def deviation(g):
                pool.wait_ge(s_mv, g + 1)
                nc.gpsimd.tensor_tensor(vareps[:, :], meanvar[:, :, 1], const["eps"][:, :].broadcast_to([P, GB]),
                                        ALU.add).then_inc(s_var, 1)
                pool.wait_ge(s_var, (2 if layer else 1) * g + 1)
                nc.gpsimd.tensor_tensor((invdev if layer else rstd)[:, :], vareps[:, :],
                                        const["power"][:, :].broadcast_to([P, GB]),
                                        ALU.pow).then_inc(s_var if layer else s_rstd, 1)
                if layer:
                    pool.wait_ge(s_var, 2 * g + 2)
                    pool.sem_inc(s_apart, 1)
                    nc.gpsimd.tensor_tensor(rstd[:, :], invdev[:, :], const["mask"][:, bass.ds(g * GB, GB)],
                                            ALU.mult).then_inc(s_rstd, 1)

            def context(g, parity, wait, values=False):
                if wait:
                    pool.wait_ge(s_fill, (g - 1) * NF + 2)
                    pool.sem_inc(s_apart, 1)
                if layer == 0:
                    nc.gpsimd.tensor_copy(ctxm[:, :, :].rearrange("p j d -> p (j d)"),
                                          step_tiles(ctx_all, g)).then_inc(s_ctx, 1)
                    return
                columns = const["mask"][:, bass.ds(g * GB, GB)]
                nc.gpsimd.tensor_tensor(ctxm[:, :, :], step_tiles(ctx_all, g).rearrange("p (j d) -> p j d", d=D),
                                        columns.unsqueeze(2).broadcast_to([P, GB, D]),
                                        ALU.mult).then_inc(s_ctx, 1)
                if values:
                    pool.wait_ge(s_pv, US * (g - 1))
                    pool.sem_inc(s_apart, 1)
                nc.gpsimd.tensor_copy(mask_g[:, parity, :], columns)
                nc.gpsimd.tensor_copy(v_hi[:, parity, :, :, HD],
                                      columns.unsqueeze(2).broadcast_to([P, GB, H])).then_inc(s_vcol, 1)

            def lower_probs(u, r):
                pool.wait_ge(s_exp_hi, u + 1)
                nc.gpsimd.tensor_tensor(p_lo[:, r, :], probs[:, r, :], p_hi[:, r, :],
                                        ALU.subtract).then_inc(s_exp_lo, 1)

            def prologue():
                context(0, 0, wait=False)
                deviation(0)

            def body(g, parity, first, last):
                for s in range(US):
                    if s == 0 and not last:
                        deviation(g + 1)
                    lower_probs(g * US + s, s % NU)
                    if s == 0 and not last:
                        context(g + 1, 1 - parity, wait=True, values=not first)

            steps(pool.Fori, prologue, body, lambda: None)


def load_and_split(nc, mem, pairs, plain):
    widest = max(hi.shape[1] for _, hi, _ in pairs)
    stage = [mem.enter_context(nc.sbuf_tensor(f"stage_{nc.next_id()}", [P, widest], F32)) for _ in range(2)]
    s_in = [mem.enter_context(nc.semaphore(f"staged_{nc.next_id()}")) for _ in pairs]
    s_plain = mem.enter_context(nc.semaphore(f"plain_{nc.next_id()}"))
    s_hi = mem.enter_context(nc.semaphore(f"split_upper_{nc.next_id()}"))
    s_lo = mem.enter_context(nc.semaphore(f"split_lower_{nc.next_id()}"))
    with nc.Block() as block:

        @block.sync
        def _(sp):
            for n, (src, hi, _) in enumerate(pairs):
                if n >= 2:
                    sp.wait_ge(s_lo, n - 1)
                sp.dma_start(shaped(stage[n % 2][:, 0:hi.shape[1]], src), src).then_inc(s_in[n], 16)
            for src, dst in plain:
                sp.dma_start(dst, src).then_inc(s_plain, 16)
            if plain:
                sp.wait_ge(s_plain, 16 * len(plain))

        @block.scalar
        def _(act):
            for n, (_, hi, _) in enumerate(pairs):
                act.wait_ge(s_in[n], 16)
                nc.scalar.activation(hi, stage[n % 2][:, 0:hi.shape[1]], ACT.Copy).then_inc(s_hi, 1)

        @block.vector
        def _(dve):
            for n, (_, hi, lo) in enumerate(pairs):
                dve.wait_ge(s_hi, n + 1)
                nc.vector.tensor_tensor(lo, stage[n % 2][:, 0:hi.shape[1]], hi.bitcast(F32),
                                        ALU.subtract).then_inc(s_lo, 1)


def shaped(tile_view, src):
    if len(src.shape) == 2:
        return tile_view
    return tile_view.rearrange("p (a b) -> p a b", b=src.shape[2])


def layer0_weights(nc, mem, bank, const, d, w, raw):
    s_raw, s_mm, s_hi, s_lo, s_lb = (mem.enter_context(nc.semaphore(n)) for n in
                                     ("raw_in", "spread_mm", "spread_hi", "spread_lo", "low_bias_done"))
    with nc.Block() as block:

        @block.sync
        def _(sp):
            for n in ("wq", "wk", "wv", "wo", "gate"):
                sp.dma_start(raw[n][:, :], d[n]).then_inc(s_raw, 16)
            sp.dma_start(raw["b"][:, 0:1], d["bq"]).then_inc(s_raw, 16)
            sp.dma_start(raw["b"][:, 1:2], d["bk"]).then_inc(s_raw, 16)

        @block.tensor
        def _(pe):
            pe.wait_ge(s_raw, 16 * 7)
            nc.tensor.matmul(bank[0][:, :], raw["wq"][:, :], const["expand"][:, :],
                             start=True, stop=True).then_inc(s_mm, 1)
            nc.tensor.matmul(bank[1][:, :], raw["wk"][:, :], const["expand"][:, :],
                             start=True, stop=True).then_inc(s_mm, 1)
            nc.tensor.transpose(bank[2][:, 0:P], raw["wv"][:, :], const["ident"][:]).then_inc(s_mm, 1)
            nc.tensor.transpose(bank[3][:, 0:E0], raw["gate"][:, :], const["ident"][0:E0, 0:E0]).then_inc(s_mm, 1)
            nc.tensor.transpose(bank[4][:, 0:P], raw["wo"][:, :], const["ident"][:]).then_inc(s_mm, 1)
            for n in range(2):
                for ch in range(4):
                    last_ = nc.tensor.matmul(bank[5][:, 4 * n + ch:4 * n + ch + 1],
                                             const["expand"][:, ch * P:(ch + 1) * P], raw["b"][:, n:n + 1],
                                             start=True, stop=True)
            last_.then_inc(s_mm, 1)

        split = [(w["wq"], 512), (w["wk"], 512), (w["wv"], P), (w["gate"], E0)]

        @block.scalar
        def _(act):
            for n, ((hi, _), width) in enumerate(split):
                act.wait_ge(s_mm, n + 1)
                nc.scalar.activation(hi[:, :], bank[n][:, 0:width], ACT.Copy).then_inc(s_hi, 1)
            act.wait_ge(s_mm, 5)
            nc.scalar.activation(w["wo"][:, 0, :], bank[4][:, 0:P], ACT.Copy)

        @block.vector
        def _(dve):
            for n, ((hi, lo), width) in enumerate(split):
                dve.wait_ge(s_hi, n + 1)
                nc.vector.tensor_tensor(lo[:, :], bank[n][:, 0:width], hi[:, :].bitcast(F32),
                                        ALU.subtract).then_inc(s_lo, 1)
            dve.wait_ge(s_mm, 6)
            nc.vector.tensor_copy(w["bias"][:, :], bank[5][:, 0:8]).then_inc(s_lb, 1)
            dve.wait_ge(s_lb, 1)
            for n in range(2):
                nc.vector.tensor_scalar(w["low_bias"][:, 4 * n:4 * n + 4], w["bias"][:, 4 * n:4 * n + 4],
                                        const["low"][:, n:n + 1], None, ALU.mult)


def ffn(nc, mem, layer, bank, x_all, const, w, out):
    ne, width, topk = (E0, I0, K0) if layer == 0 else (E1, I1, K1)
    nc_ = ne * width // P + (0 if layer == 0 else HS // P)
    half = 32 if layer == 0 else 16
    nt = GB
    T = B * S

    def sb(name, shape, dt=F32):
        return mem.enter_context(nc.sbuf_tensor(f"{name}_f{layer}", shape, dt))

    def sem(name):
        return mem.enter_context(nc.semaphore(f"{name}_f{layer}"))

    def early(name, shape, dt=F32):
        return routing.enter_context(nc.sbuf_tensor(f"{name}_f{layer}", shape, dt))

    ident = const["ident"]
    x_hi, x_lo = sb("x_hi", [P, T], F32R), sb("x_lo", [P, T], F32R)
    comb_t = sb("comb_t", [2 * half, T], F32R)
    routing = ExitStack()
    comb_up = early("comb_up", [2 * half, 2, 512], F32R)
    xhat = early("xhat", [P, 2, nt, D])
    stats = early("stats", [P, 2, nt, 6])
    meanvar = early("meanvar", [P, 2, nt, 2])
    vareps = early("vareps", [P, 2, nt])
    rstd = early("rstd", [P, 2, nt])
    score = early("score", [P, B, ne])
    biased = early("biased", [P, B, ne + 4])
    top8 = early("top8", [P, B, 8])
    top = early("top", [P, B, 8])
    marked = early("marked", [P, B, ne + 4])
    total = early("total", [P, B])
    comb = early("comb", [P, B, 2 * half])

    s_stats, s_mv, s_var, s_rstd, s_xhat = (sem(n) for n in ("stats", "mv", "var", "rstd", "xhat"))
    s_tr, s_up, s_low, s_route = sem("tr"), sem("up"), sem("low"), sem("route")

    def cols(t, g):
        return t[:, bass.ds(g * 512, 512)]

    def tiles(t, g):
        return t[:, bass.ds(g * nt * D, nt * D)]

    LB = bank[6], bank[7]

    with nc.Block() as block:

        @block.tensor
        def _(pe):
            def logits(g, i):
                pe.wait_ge(s_low, g + 1)
                for t in range(nt):
                    n = g * nt + t
                    o = LB[n * ne // 512][:, n * ne % 512:n * ne % 512 + ne]
                    a = slice(n * P, (n + 1) * P)
                    nc.tensor.matmul(o, x_hi[:, a], w["gate"][0][:, :], start=True, stop=False)
                    nc.tensor.matmul(o, x_hi[:, a], w["gate"][1][:, :], start=False, stop=False)
                    last_ = nc.tensor.matmul(o, x_lo[:, a], w["gate"][0][:, :], start=False, stop=True)
                last_.then_inc(s_route, 1)

            for g in range(G):
                pe.wait_ge(s_xhat, g + 1)
                if g >= 2:
                    pe.wait_ge(s_low, g - 1)
                for t in range(nt):
                    last_ = nc.tensor.transpose(bank[g % 2][:, t * P:(t + 1) * P], xhat[:, g % 2, t, :], ident[:])
                last_.then_inc(s_tr, 1)
                if g >= 1:
                    logits(g - 1, 0)
            logits(G - 1, 0)

        @block.scalar
        def _(act):
            for g in range(G):
                act.wait_ge(s_tr, g + 1)
                nc.scalar.activation(x_hi[:, g * 512:(g + 1) * 512], bank[g % 2][:, :], ACT.Copy).then_inc(s_up, 1)
            act.wait_ge(s_route, G)
            for n in range(0, B * ne, 512):
                m = min(512, B * ne)
                nc.scalar.activation(score[:, n // ne:(n + m) // ne, :],
                                     LB[n // 512][:, 0:m].rearrange("p (a b) -> p a b", b=ne), ACT.Sigmoid)

        @block.vector
        def _(dve):
            def norm(g):
                for t in range(nt):
                    last_ = nc.vector.bn_stats(stats[:, g % 2, t, :], x_all[:, (g * nt + t) * D:(g * nt + t + 1) * D])
                last_.then_inc(s_stats, 1)
                dve.wait_ge(s_stats, g + 1)
                for t in range(nt):
                    last_ = nc.vector.bn_aggr(meanvar[:, g % 2, t, :], stats[:, g % 2, t, :])
                last_.then_inc(s_mv, 1)

            def lower(g):
                dve.wait_ge(s_up, g + 1)
                nc.vector.tensor_tensor(x_lo[:, g * 512:(g + 1) * 512], bank[g % 2][:, :],
                                        x_hi[:, g * 512:(g + 1) * 512].bitcast(F32), ALU.subtract).then_inc(s_low, 1)

            norm(0)
            for g in range(G):
                if g + 1 < G:
                    norm(g + 1)
                dve.wait_ge(s_rstd, g + 1)
                if g >= 2:
                    dve.wait_ge(s_tr, g - 1)
                for t in range(nt):
                    last_ = nc.vector.tensor_scalar(xhat[:, g % 2, t, :],
                                                    x_all[:, (g * nt + t) * D:(g * nt + t + 1) * D],
                                                    meanvar[:, g % 2, t, 0:1], rstd[:, g % 2, t:t + 1],
                                                    ALU.subtract, ALU.mult)
                last_.then_inc(s_xhat, 1)
                if g >= 1:
                    lower(g - 1)
            lower(G - 1)

        @block.gpsimd
        def _(pool):
            for g in range(G):
                pool.wait_ge(s_mv, g + 1)
                nc.gpsimd.tensor_scalar(vareps[:, g % 2, :], meanvar[:, g % 2, :, 1], EPS, None,
                                        ALU.add).then_inc(s_var, 1)
                pool.wait_ge(s_var, g + 1)
                nc.gpsimd.tensor_tensor(rstd[:, g % 2, :], vareps[:, g % 2, :],
                                        const["power"][:, :].broadcast_to([P, nt]), ALU.pow).then_inc(s_rstd, 1)

    s_c, s_ct, s_cu = sem("choice"), sem("comb_tr"), sem("comb_up")
    s_comb = sem("comb")
    with nc.Block() as block:

        @block.vector
        def _(dve):
            done = [0]

            def after(instruction):
                done[0] += 1
                instruction.then_inc(s_c, 1)
                dve.wait_ge(s_c, done[0])

            nc.vector.memset(biased[:, :, ne:ne + 4], NONE)
            nc.vector.memset(top[:, :, topk:8], NONE)
            if layer == 0:
                after(nc.vector.tensor_tensor(biased[:, :, 0:ne], score[:, :, :],
                                              w["ebias"][:, :].unsqueeze(1).broadcast_to([P, B, ne]), ALU.add))
            else:
                after(nc.vector.tensor_copy(biased[:, :, 0:ne], score[:, :, :]))
                nc.vector.memset(top[:, :, topk:8], NONE)
            for t in range(B):
                last_ = nc.vector.max(top8[:, t, :], biased[:, t, 0:ne])
            after(last_)
            after(nc.vector.tensor_copy(top[:, :, 0:topk], top8[:, :, 0:topk]))
            for t in range(B):
                last_ = nc.vector.match_replace(marked[:, t, :], top[:, t, :], biased[:, t, :], 2.0 * NONE)
            after(last_)
            after(nc.vector.tensor_single_scalar(comb[:, :, 0:ne], marked[:, :, 0:ne], 1.5 * NONE, ALU.is_lt))
            after(nc.vector.tensor_tensor(score[:, :, :], comb[:, :, 0:ne], score[:, :, :], ALU.mult))
            after(nc.vector.tensor_reduce(total[:, :], score[:, :, :], AX.X, ALU.add))
            after(nc.vector.reciprocal(total[:, :], total[:, :]))
            for h in range(2):
                if layer:
                    nc.vector.memset(comb[:, :, h * half + ne:h * half + half], 1.0)
                last_ = nc.vector.tensor_tensor(comb[:, :, h * half:h * half + ne], score[:, :, :],
                                                total[:, :].unsqueeze(2).broadcast_to([P, B, ne]), ALU.mult)
            last_.then_inc(s_comb, 1)
            for g in range(G):
                dve.wait_ge(s_cu, g + 1)
                nc.vector.tensor_tensor(comb_t[:, g * 512:(g + 1) * 512], bank[g % 2][0:2 * half, :],
                                        comb_up[:, g % 2, :].bitcast(F32), ALU.subtract).then_inc(s_ct, 1)

        @block.tensor
        def _(pe):
            pe.wait_ge(s_comb, 1)
            for g in range(G):
                if g >= 2:
                    pe.wait_ge(s_ct, g - 1)
                for t in range(nt):
                    last_ = nc.tensor.transpose(bank[g % 2][0:2 * half, t * P:(t + 1) * P],
                                                comb[:, g * nt + t, :], ident[:])
                last_.then_inc(s_tr, 1)

        @block.scalar
        def _(act):
            for g in range(G):
                act.wait_ge(s_tr, G + g + 1)
                if g >= 2:
                    act.wait_ge(s_ct, g - 1)
                nc.scalar.activation(comb_up[:, g % 2, :], bank[g % 2][0:2 * half, :], ACT.Copy,
                                     scale=const[f"low_comb{layer}"][:, :]).then_inc(s_cu, 1)

    routing.close()
    gate_act = sb("gate_act", [P, 2, 512])
    hidden = sb("hidden", [P, 2, 512])
    weighted = sb("weighted", [P, 2, 512])
    ring = 3 if layer == 0 else 5
    assert 2 * nc_ % ring == 0
    w_hi, w_lo = sb("w_hi", [P, ring, 512], F32R), sb("w_lo", [P, ring, 512], F32R)
    y_t = sb("y_t", [P, 2, 512])
    s_g, s_silu, s_u, s_cm, s_a, s_wh, s_wl, s_y, s_yt, s_ytr, s_x, s_hid = (
        sem(n) for n in ("gate_mm", "silu", "up_mm", "comb_mm", "weighed", "weighed_hi", "weighed_lo", "down", "y_t",
                         "y_tr", "x", "hid"))
    s_store = sem("store")
    GATE, UP, CB, YB, TB = [bank[0], bank[1]], [bank[2], bank[3]], [bank[4], bank[5]], bank[6], bank[7]

    def steps(loop, body):
        body(0, 0, True)
        body(1, 1, False)
        with loop(1, G // 2) as pair:
            body(2 * pair, 0, False)
            body(2 * pair + 1, 1, False)

    with nc.Block() as block:

        @block.tensor
        def _(pe):
            def up(g, k, parity, first):
                n = (parity * nc_ + k) % 2
                x1, x2 = cols(x_hi, g), cols(x_lo, g)
                a = slice(k * P, (k + 1) * P)
                if not (first and k < 2):
                    pe.wait_ge(s_silu, g * nc_ + k - 1)
                for (hi, lo), dst, done in ((w["w1"], GATE[n], s_g), (w["w3"], UP[n], s_u)):
                    if done is s_u and not (first and k < 2):
                        pe.wait_ge(s_hid, g * nc_ + k - 1)
                    nc.tensor.matmul(dst[:, :], hi[:, a], x1, start=True, stop=False)
                    nc.tensor.matmul(dst[:, :], lo[:, a], x1, start=False, stop=False)
                    nc.tensor.matmul(dst[:, :], hi[:, a], x2, start=False, stop=True).then_inc(done, 1)
                pe.wait_ge(const["s_power"], 1)
                if not (first and k < 2):
                    pe.wait_ge(s_a, g * nc_ + k - 1)
                nc.tensor.matmul(CB[n][:, :], const[f"pick{layer}"][:, k, :], cols(comb_t, g),
                                 start=True, stop=True).then_inc(s_cm, 1)

            def down(g, k, parity, first):
                slot = (parity * nc_ + k) % ring
                pe.wait_ge(s_wl, g * nc_ + k + 1)
                if k == 0 and not first:
                    pe.wait_ge(s_yt, g)
                a = slice(k * P, (k + 1) * P)
                hi, lo = w["w2"]
                nc.tensor.matmul(YB[:, :], hi[:, a], w_hi[:, slot, :], start=(k == 0), stop=False)
                nc.tensor.matmul(YB[:, :], lo[:, a], w_hi[:, slot, :], start=False, stop=False)
                nc.tensor.matmul(YB[:, :], hi[:, a], w_lo[:, slot, :], start=False,
                                 stop=(k == nc_ - 1)).then_inc(s_y, 1)

            def back(g, parity, first):
                pe.wait_ge(s_yt, g + 1)
                if not first:
                    pe.wait_ge(s_x, g)
                for t in range(nt):
                    last_ = nc.tensor.transpose(TB[:, t * P:(t + 1) * P], y_t[:, parity, t * P:(t + 1) * P], ident[:])
                last_.then_inc(s_ytr, 1)

            def body(g, parity, first):
                for k in range(nc_):
                    up(g, k, parity, first)
                    if k == 2 and not first:
                        back(g - 1, 1 - parity, isinstance(g, int) and g == 1)
                    if k >= 2:
                        down(g, k - 2, parity, first)
                    elif not first:
                        down(g - 1, nc_ + k - 2, 1 - parity, False)

            steps(pe.Fori, body)
            for k in range(nc_ - 2, nc_):
                down(G - 1, k, 1, False)
            back(G - 1, 1, False)

        @block.scalar
        def _(act):
            def upper(g, k, parity, first):
                n, slot = g * nc_ + k, (parity * nc_ + k) % ring
                act.wait_ge(s_a, n + 1)
                if not (first and k < ring):
                    act.wait_ge(s_y, n - ring + 1)
                nc.scalar.activation(w_hi[:, slot, :], weighted[:, (parity * nc_ + k) % 2, :],
                                     ACT.Copy).then_inc(s_wh, 1)

            def result(g, parity, first):
                act.wait_ge(s_y, g * nc_ + nc_)
                if not first:
                    act.wait_ge(s_ytr, g)
                nc.scalar.activation(y_t[:, parity, :], YB[:, :], ACT.Copy).then_inc(s_yt, 1)

            def body(g, parity, first):
                for k in range(nc_):
                    n, slot = g * nc_ + k, (parity * nc_ + k) % 2
                    act.wait_ge(s_g, n + 1)
                    if not (first and k < 2):
                        act.wait_ge(s_hid, n - 1)
                    nc.scalar.activation(gate_act[:, slot, :], GATE[slot][:, :], ACT.Silu).then_inc(s_silu, 1)
                    if k:
                        upper(g, k - 1, parity, first)
                    elif not first:
                        upper(g - 1, nc_ - 1, 1 - parity, False)
                    if k == 1 and not first:
                        result(g - 1, 1 - parity, isinstance(g, int) and g == 1)

            steps(act.Fori, body)
            upper(G - 1, nc_ - 1, 1, False)
            result(G - 1, 1, False)

        @block.vector
        def _(dve):
            def add(g):
                dve.wait_ge(s_ytr, g + 1)
                nc.vector.tensor_tensor(tiles(x_all, g), TB[:, :], tiles(x_all, g), ALU.add).then_inc(s_x, 1)

            def body(g, parity, first):
                for k in range(nc_):
                    n, slot = g * nc_ + k, (parity * nc_ + k) % 2
                    dve.wait_ge(s_silu, n + 1)
                    dve.wait_ge(s_u, n + 1)
                    nc.vector.tensor_tensor(hidden[:, slot, :], UP[slot][:, :], gate_act[:, slot, :],
                                            ALU.mult).then_inc(s_hid, 1)
                    dve.wait_ge(s_hid, n + 1)
                    dve.wait_ge(s_cm, n + 1)
                    if not (first and k < 2):
                        dve.wait_ge(s_wl, n - 1)
                    nc.vector.tensor_tensor(weighted[:, slot, :], CB[slot][:, :], hidden[:, slot, :],
                                            ALU.mult).then_inc(s_a, 1)
                    if k == 3 and not first:
                        add(g - 1)

            steps(dve.Fori, body)
            add(G - 1)

        @block.gpsimd
        def _(pool):
            def body(g, parity, first):
                for k in range(nc_):
                    n, slot = g * nc_ + k, (parity * nc_ + k) % ring
                    pool.wait_ge(s_wh, n + 1)
                    nc.gpsimd.tensor_tensor(w_lo[:, slot, :], weighted[:, (parity * nc_ + k) % 2, :],
                                            w_hi[:, slot, :].bitcast(F32), ALU.subtract).then_inc(s_wl, 1)

            steps(pool.Fori, body)

        if out is not None:
            @block.sync
            def _(sp):
                for g in range(G):
                    sp.wait_ge(s_x, g + 1)
                    sp.dma_start(out[:, g * GB:(g + 1) * GB, :],
                                 x_all[:, g * GB * D:(g + 1) * GB * D].rearrange("p (b d) -> p b d", d=D)).then_inc(s_store, 16)
                sp.wait_ge(s_store, 16 * G)


def program(nc, a, out):
    with ExitStack() as mem:
        def sb(name, shape, dt=F32):
            return mem.enter_context(nc.sbuf_tensor(name, shape, dt))

        bank = [mem.enter_context(nc.psum_tensor(f"bank{i}", [P, 512], F32)) for i in range(8)]
        x_all = sb("x_all", [P, B * D])
        ctx_all = sb("ctx_all", [P, B * D])
        const = {
            "ident": sb("ident", [P, P]), "power": sb("power", [P, 1]), "ones": sb("ones", [1, P]), "eps": sb("eps", [P, 1]),
            "low": sb("low", [P, 2]), "quarter": sb("quarter", [P, 4]), "mask": sb("mask", [P, B]),
            "low_comb0": sb("low_comb0", [64, 1]), "low_comb1": sb("low_comb1", [32, 1]),
        }
        gate0 = sb("gate0_hi", [P, E0], F32R), sb("gate0_lo", [P, E0], F32R)
        s_in, s_mk = (mem.enter_context(nc.semaphore(n)) for n in ("inputs", "mask_tr"))
        const["s_power"] = mem.enter_context(nc.semaphore("power_set"))

        def rounded(name, shape, dram, scope):
            t = scope.enter_context(nc.sbuf_tensor(name, shape, F16))
            raw_ = scope.enter_context(nc.sbuf_tensor(name + "_raw", shape, F32))
            s1, s2 = (scope.enter_context(nc.semaphore(f"{name}_{i}")) for i in range(2))
            with nc.Block() as block:

                @block.sync
                def _(sp):
                    sp.dma_start(raw_[:], dram).then_inc(s1, 16)

                @block.scalar
                def _(act):
                    act.wait_ge(s1, 16)
                    nc.scalar.activation(t[:], raw_[:], ACT.Copy)
            return t

        maskt = sb("mask_rows", [B, P])
        with nc.Block() as block:

            @block.sync
            def _(sp):
                for dst, src in ((const["ident"][:, :], a["c_ident"]), (maskt[:, :], a["mask_BxS2_fk1"]),
                                 (const["low"][:, :], a["c_low"]), (const["quarter"][:, :], a["c_quarter"]), (const["low_comb0"][:, :], a["c_low_comb0"]),
                                 (const["low_comb1"][:, :], a["c_low_comb1"]),
                                 (x_all[:, :].rearrange("p (b d) -> p b d", d=D), a["x"].rearrange("b s d -> s b d")),
                                 (ctx_all[:, :].rearrange("p (b d) -> p b d", d=D),
                                  a["ctx_1024"].rearrange("b s d -> s b d"))):
                    sp.dma_start(dst, src).then_inc(s_in, 16)

            @block.tensor
            def _(pe):
                pe.wait_ge(s_in, 16 * 8)
                nc.tensor.transpose(bank[0][:, 0:B], maskt[:, :], const["ident"][0:B, 0:B]).then_inc(s_mk, 1)

            @block.vector
            def _(dve):
                nc.vector.memset(const["eps"][:, :], EPS)
                nc.vector.memset(const["ones"][:, :], 1.0)
                nc.vector.memset(const["power"][:, :], -0.5).then_inc(const["s_power"], 1)
                dve.wait_ge(s_mk, 1)
                nc.vector.tensor_copy(const["mask"][:, :], bank[0][:, 0:B])

        with ExitStack() as scope:
            def sc(name, shape, dt=F32):
                return scope.enter_context(nc.sbuf_tensor(name, shape, dt))

            const["sel"] = rounded("sel0", [P, H, P], a["c_sel0"], scope)
            const["expand"] = sc("expand", [P, 512])
            w = {"wq": (sc("wq0_hi", [P, 512], F32R), sc("wq0_lo", [P, 512], F32R)),
                 "wk": (sc("wk0_hi", [P, 512], F32R), sc("wk0_lo", [P, 512], F32R)),
                 "wv": (sc("wv0_hi", [P, D], F32R), sc("wv0_lo", [P, D], F32R)),
                 "wo": sc("wo0", [P, 1, D]), "bias": sc("bias0", [P, 8]), "low_bias": sc("low_bias0", [P, 8]),
                 "bv": sc("bv0", [1, D]), "bo": sc("bo0", [1, D]), "gate": gate0}
            raw = {n: sc(f"raw_{n}", [P, P]) for n in ("wq", "wk", "wv", "wo")}
            raw["gate"], raw["b"] = sc("raw_gate", [E0, P]), sc("raw_b", [P, 2])
            load_and_split_plain(nc, scope, ((a["c_expand"], const["expand"][:, :]),
                                             (a["L0_xattn_bv"].unsqueeze(0), w["bv"][:, :]),
                                             (a["L0_xattn_bo"].unsqueeze(0), w["bo"][:, :])))
            layer0_weights(nc, scope, bank, const,
                           {"wq": a["L0_xattn_Wq"], "wk": a["L0_xattn_Wk"], "wv": a["L0_xattn_Wv"],
                            "wo": a["L0_xattn_Wo"], "gate": a["L0_ffn_gate_w"],
                            "bq": a["L0_xattn_bq"].unsqueeze(1), "bk": a["L0_xattn_bk"].unsqueeze(1)}, w, raw)
            attention(nc, scope, 0, bank, x_all, ctx_all, const, w)

        with ExitStack() as scope:
            def sc(name, shape, dt=F32):
                return scope.enter_context(nc.sbuf_tensor(name, shape, dt))

            n0 = E0 * I0
            w = {"w1": (sc("w1_hi", [P, n0], F32R), sc("w1_lo", [P, n0], F32R)),
                 "w3": (sc("w3_hi", [P, n0], F32R), sc("w3_lo", [P, n0], F32R)),
                 "w2": (sc("w2_hi", [P, n0], F32R), sc("w2_lo", [P, n0], F32R)), "ebias": sc("ebias", [P, E0]), "gate": gate0}
            with ExitStack() as staging:
                const["pick0"] = scope.enter_context(nc.sbuf_tensor("pick0", [64, n0 // P, P], F32R))
                load_and_split(nc, staging,
                               [(a["L0_ffn_w1"].rearrange("e h i -> h e i"), w["w1"][0][:, :], w["w1"][1][:, :]),
                                (a["L0_ffn_w3"].rearrange("e h i -> h e i"), w["w3"][0][:, :], w["w3"][1][:, :]),
                                (a["L0_ffn_w2"].rearrange("e i h -> (e i) h").rearrange("(c p) h -> p c h", p=P),
                                 w["w2"][0][:, :], w["w2"][1][:, :])],
                               [(a["L0_ffn_e_bias"].partition_broadcast(P), w["ebias"][:, :])])
                round_constant(nc, staging, const["pick0"], "pick0", a["c_pick0"])
            ffn(nc, scope, 0, bank, x_all, const, w, None)

        with ExitStack() as scope:
            def sc(name, shape, dt=F32):
                return scope.enter_context(nc.sbuf_tensor(name, shape, dt))

            w = {n: (sc(f"{n}1_hi", [P, H * D1], F32R), sc(f"{n}1_lo", [P, H * D1], F32R)) for n in ("wq", "wk", "wv")}
            w["wo"] = sc("wo1", [P, H * D1 // P, D])
            const["sel"] = scope.enter_context(nc.sbuf_tensor("sel1", [P, 8, P], F16))
            with ExitStack() as staging:
                load_and_split(nc, staging,
                               [(a[f"L1_xattn_{m}"], w[n][0][:, :], w[n][1][:, :])
                                for n, m in (("wq", "Wq"), ("wk", "Wk"), ("wv", "Wv"))],
                               [(a["L1_xattn_Wo"].rearrange("(c p) h -> p c h", p=P), w["wo"][:, :, :])])
                round_constant(nc, staging, const["sel"], "sel1", a["c_sel1"])
            attention(nc, scope, 1, bank, x_all, ctx_all, const, w)

        with ExitStack() as scope:
            def sc(name, shape, dt=F32):
                return scope.enter_context(nc.sbuf_tensor(name, shape, dt))

            n1 = E1 * I1 + HS
            nr = E1 * I1
            w = {n: (sc(f"{n}f_hi", [P, n1], F32R), sc(f"{n}f_lo", [P, n1], F32R)) for n in ("w1", "w3", "w2")}
            w["gate"] = sc("gate1_hi", [P, E1], F32R), sc("gate1_lo", [P, E1], F32R)
            const["pick1"] = scope.enter_context(nc.sbuf_tensor("pick1", [32, n1 // P, P], F32R))
            with ExitStack() as staging:
                pairs = []
                for n in ("1", "3"):
                    hi, lo = w["w" + n]
                    pairs.append((a["L1_ffn_w" + n].rearrange("e h i -> h e i"), hi[:, 0:nr], lo[:, 0:nr]))
                    pairs.append((a["L1_ffn_ws" + n], hi[:, nr:n1], lo[:, nr:n1]))
                pairs.append((a["L1_ffn_gate_w"], w["gate"][0][:, :], w["gate"][1][:, :]))
                hi, lo = w["w2"]
                pairs.append((a["L1_ffn_w2"].rearrange("e i h -> (e i) h").rearrange("(c p) h -> p c h", p=P),
                              hi[:, 0:nr], lo[:, 0:nr]))
                pairs.append((a["L1_ffn_ws2"], hi[:, nr:n1], lo[:, nr:n1]))
                load_and_split(nc, staging, pairs, [])
                round_constant(nc, staging, const["pick1"], "pick1", a["c_pick1"])
            ffn(nc, scope, 1, bank, x_all, const, w, out.rearrange("b s d -> s b d"))


def load_and_split_plain(nc, mem, plain):
    s = mem.enter_context(nc.semaphore(f"plain_in_{nc.next_id()}"))
    with nc.Block() as block:

        @block.sync
        def _(sp):
            for src, dst in plain:
                sp.dma_start(dst, src).then_inc(s, 16)
            sp.wait_ge(s, 16 * len(plain))


def round_constant(nc, mem, t, name, dram):
    raw = mem.enter_context(nc.sbuf_tensor(name + "_raw", list(t.shape), F32))
    s = mem.enter_context(nc.semaphore(name + "_in"))
    with nc.Block() as block:

        @block.sync
        def _(sp):
            sp.dma_start(raw[:], dram).then_inc(s, 16)

        @block.scalar
        def _(act):
            act.wait_ge(s, 16)
            nc.scalar.activation(t[:], raw[:], ACT.Copy)


def constants():
    f = np.float32
    ident = np.eye(P, dtype=f)
    expand = np.zeros((P, 512), f)
    for h in range(H):
        ch, part = divmod(h, 4)
        for term in range(4):
            for d in range(D0):
                expand[h * D0 + d, ch * P + part * 32 + term * D0 + d] = 1
    term = np.arange(P) % 32 // D0
    low = np.stack([term >= 2, term % 2 == 1], 1).astype(f)
    rows = np.arange(P)
    sel0 = np.zeros((P, H, P), f)
    sel1 = np.zeros((P, 8, P), f)
    for m in range(H):
        sel0[m, m, :] = 1
    for m in range(8):
        sel1[rows % 64 == m, m, :] = 1
    pick0 = np.zeros((64, E0 * I0 // P, P), f)
    for n in range(E0 * I0):
        for h in range(2):
            pick0[h * 32 + n // I0, n // P, n % P] = 1
    pick1 = np.zeros((32, (E1 * I1 + HS) // P, P), f)
    for n in range(E1 * I1 + HS):
        e = n // I1 if n < E1 * I1 else E1
        for h in range(2):
            pick1[h * 16 + e, n // P, n % P] = 1
    return {"c_ident": ident, "c_expand": expand, "c_low": low, "c_quarter": (rows[:, None] // 32 == np.arange(4)).astype(f), "c_sel0": sel0, "c_sel1": sel1,
            "c_pick0": pick0, "c_pick1": pick1,
            "c_low_comb0": (np.arange(64) >= 32).astype(f)[:, None],
            "c_low_comb1": (np.arange(32) >= 16).astype(f)[:, None]}


def kernel(**inputs):
    import concourse.bacc as bacc
    from concourse.bass_utils import run_bass_kernel_spmd

    nc = bacc.Bacc("TRN2", target_bir_lowering=False, num_devices=1)
    arrays = {n: np.ascontiguousarray(v) for n, v in inputs.items()}
    arrays.update(constants())
    args = {n: nc.dram_tensor(n, v.shape, F32, kind="ExternalInput").ap() for n, v in arrays.items()}
    out = nc.dram_tensor("out", (B, S, D), F32, kind="ExternalOutput").ap()
    program(nc, args, out)
    r = run_bass_kernel_spmd(nc, [arrays], core_ids=[0])
    return r.results[0]["out"]
```
